# Optimizing a Trainium2 kernel written in Bass

```python
import numpy as np
import jax
import jax.numpy as jnp

def _softmax(x, axis=-1):
    return jax.nn.softmax(x, axis=axis)

def _gelu(x):
    return jax.nn.gelu(x, approximate=True)

def _silu(x):
    return jax.nn.silu(x)

def _sigmoid(x):
    return jax.nn.sigmoid(x)

def _layernorm(x, axis=-1, eps=1e-05):
    m = jnp.mean(x, axis=axis, keepdims=True)
    v = jnp.var(x, axis=axis, keepdims=True)
    return (x - m) / jnp.sqrt(v + eps)

def _scatter_add(tgt, idx, src, axis=0):
    return tgt.at[idx].add(src)

def _segment_sum(src, seg, n):
    return jax.ops.segment_sum(src, seg, n)
kernel_name = 'mk_decoder_postln_d1_seqx_r8_1e11f3'

def setup_inputs(seed: int=0):
    np.random.seed(seed)
    _w = jnp.asarray

    def _rec_inputs():
        import jax
        import jax.numpy as jnp
        _rk = jax.random.key(seed)
        x = -0.0002928 + 1 * jax.random.normal(jax.random.fold_in(_rk, 1), (32, 64, 256), jnp.float32)
        _lenS = 64 - jax.random.randint(jax.random.fold_in(_rk, 7), (32,), 0, max(1, 64 // 4) + 1, jnp.int32)
        _lenS2 = 64 - jax.random.randint(jax.random.fold_in(_rk, 8), (32,), 0, max(1, 64 // 4) + 1, jnp.int32)
        _ctx_512P = jax.random.normal(jax.random.fold_in(_rk, 11), (32, 16, 64), jnp.float32)
        _ctx_512c = jax.random.dirichlet(jax.random.fold_in(_rk, 511), 0.3 * jnp.ones((16,), jnp.float32), (32, 64))
        _ctx_512t = jnp.einsum('bsk,bkd->bsd', _ctx_512c, _ctx_512P)
        _ctx_512t = _ctx_512t * jax.lax.rsqrt(jnp.mean(jnp.square(_ctx_512t)) + 1e-12) * 0.953939
        ctx_512 = 0.000227908 + 0.99994 * (_ctx_512t + 0.3 * jax.random.normal(jax.random.fold_in(_rk, 611), (32, 64, 64), jnp.float32))
        return (x, ctx_512)
    x, ctx_512 = _rec_inputs()

    def _L0_attn_setup():
        import jax, jax.numpy as jnp
        import numpy as np
        NUM_STEPS = 3
        NUM_HEADS = 8
        HEAD_DIM = 128
        EPS = 1e-05

        def layernorm(x, g, b):
            mu = jnp.mean(x, -1, keepdims=True)
            var = jnp.mean(jnp.square(x - mu), -1, keepdims=True)
            return (x - mu) * jax.lax.rsqrt(var + EPS) * g + b

        def entmax15(x):
            x = (x - jnp.max(x, -1, keepdims=True)) / 2.0
            xs = jnp.flip(jnp.sort(x, -1), -1)
            rho = jnp.arange(1, x.shape[-1] + 1, dtype=x.dtype)
            mean = jnp.cumsum(xs, -1) / rho
            meansq = jnp.cumsum(xs * xs, -1) / rho
            ss = rho * (meansq - jnp.square(mean))
            tau = mean - jnp.sqrt(jnp.clip((1.0 - ss) / rho, 0.0, None))
            support = jnp.sum(tau <= xs, -1, keepdims=True)
            tau_star = jnp.take_along_axis(tau, support - 1, -1)
            return jnp.square(jnp.clip(x - tau_star, 0.0, None))
        key = jax.random.key(seed)
        ks = jax.random.split(key, 6)
        B, S, Hd, Md, N = (2, 128, 256, 128, 256)
        THD = NUM_HEADS * HEAD_DIM
        return {'hidden': jax.random.normal(ks[0], (B, S, Hd), jnp.float32), 'memory': jax.random.normal(ks[1], (N, Md), jnp.float32), 'Wq': jax.random.normal(ks[2], (THD, Hd), jnp.float32) / np.float32(np.sqrt(Hd)), 'Wk': jax.random.normal(ks[3], (THD, Md), jnp.float32) / np.float32(np.sqrt(Md)), 'Wv': jax.random.normal(ks[4], (THD, Md), jnp.float32) / np.float32(np.sqrt(Md)), 'Wo': jax.random.normal(ks[5], (Hd, THD), jnp.float32) / np.float32(np.sqrt(THD)), 'log_beta': jnp.full((NUM_HEADS,), float(np.log(1.0 / np.sqrt(HEAD_DIM))), jnp.float32), 'g_state': jnp.ones((Hd,), jnp.float32), 'b_state': jnp.zeros((Hd,), jnp.float32), 'g_mem': jnp.ones((Md,), jnp.float32), 'b_mem': jnp.zeros((Md,), jnp.float32)}
    _L0_attn_all = _L0_attn_setup()
    _L0_attn_in = {k: v for k, v in _L0_attn_all.items() if k in ('memory', 'Wq', 'Wk', 'Wv', 'Wo', 'log_beta', 'g_state', 'b_state', 'g_mem', 'b_mem')}
    del _L0_attn_all

    def _L0_xattn_setup():
        import jax, jax.numpy as jnp
        import numpy as np
        B, S, L = (2, 128, 128)
        DIM_Q, H, K, D_C, D_CQ, R = (256, 16, 128, 64, 192, 64)

        def _rope_tables(seq_len, dim, dtype):
            inv_freq = 1.0 / 10000.0 ** (jnp.arange(0, dim, 2, dtype=dtype) / dim)
            t = jnp.arange(seq_len, dtype=dtype)
            freqs = t[:, None] * inv_freq[None, :]
            sin = jnp.repeat(jnp.sin(freqs), 2, axis=-1)
            cos = jnp.repeat(jnp.cos(freqs), 2, axis=-1)
            return (sin, cos)

        def _rotate_half(x):
            h = x.shape[-1] // 2
            return jnp.concatenate([-x[..., h:], x[..., :h]], axis=-1)
        key = jax.random.key(seed)
        ks = jax.random.split(key, 8)
        s_in = 1.0 / np.sqrt(DIM_Q)
        s_k = 1.0 / np.sqrt(K)
        s_cq = 1.0 / np.sqrt(D_CQ)
        s_c = 1.0 / np.sqrt(D_C)
        return {'hidden_q': jax.random.normal(ks[0], (B, S, DIM_Q), jnp.float32), 'kv_c': jax.random.normal(ks[1], (B, L, D_C), jnp.float32), 'Wq': jax.random.normal(ks[2], (H * K, DIM_Q), jnp.float32) * s_in, 'w_kc_q': jax.random.normal(ks[3], (H, K, D_CQ), jnp.float32) * s_k, 'w_kc_kv': jax.random.normal(ks[4], (H, K, D_C), jnp.float32) * s_k, 'W_qr': jax.random.normal(ks[5], (H, D_CQ, R), jnp.float32) * s_cq / np.sqrt(R), 'W_kr': jax.random.normal(ks[6], (H, D_C, R), jnp.float32) * s_c, 'Wo': jax.random.normal(ks[7], (DIM_Q, H * K), jnp.float32) * s_k}
    _L0_xattn_all = _L0_xattn_setup()
    _L0_xattn_in = {k: v for k, v in _L0_xattn_all.items() if k in ('Wq', 'w_kc_q', 'w_kc_kv', 'W_qr', 'W_kr', 'Wo')}
    del _L0_xattn_all

    def _L0_ffn_setup():
        import jax, jax.numpy as jnp
        import numpy as np
        key = jax.random.key(seed)
        k1, k2, k3, k4 = jax.random.split(key, 4)
        B, S, D_IN, D_OUT = (4, 512, 256, 256)
        x = jax.random.normal(k1, (B, S, D_IN), dtype=jnp.float32)
        weight = jax.random.normal(k2, (D_OUT, D_IN), dtype=jnp.float32) * 0.02
        scale_weight = jax.random.uniform(k3, (D_OUT,), dtype=jnp.float32, minval=0.5, maxval=1.5)
        bias = jax.random.normal(k4, (D_OUT,), dtype=jnp.float32) * 0.02
        return {'x': x, 'weight': weight, 'scale_weight': scale_weight, 'bias': bias}
    _L0_ffn_all = _L0_ffn_setup()
    _L0_ffn_in = {k: v for k, v in _L0_ffn_all.items() if k in ('weight', 'scale_weight', 'bias')}
    del _L0_ffn_all
    return {'x': x, 'ctx_512': ctx_512, 'L0_attn_memory': _L0_attn_in['memory'], 'L0_attn_Wq': _L0_attn_in['Wq'], 'L0_attn_Wk': _L0_attn_in['Wk'], 'L0_attn_Wv': _L0_attn_in['Wv'], 'L0_attn_Wo': _L0_attn_in['Wo'], 'L0_attn_log_beta': _L0_attn_in['log_beta'], 'L0_attn_g_state': _L0_attn_in['g_state'], 'L0_attn_b_state': _L0_attn_in['b_state'], 'L0_attn_g_mem': _L0_attn_in['g_mem'], 'L0_attn_b_mem': _L0_attn_in['b_mem'], 'L0_xattn_Wq': _L0_xattn_in['Wq'], 'L0_xattn_w_kc_q': _L0_xattn_in['w_kc_q'], 'L0_xattn_w_kc_kv': _L0_xattn_in['w_kc_kv'], 'L0_xattn_W_qr': _L0_xattn_in['W_qr'], 'L0_xattn_W_kr': _L0_xattn_in['W_kr'], 'L0_xattn_Wo': _L0_xattn_in['Wo'], 'L0_ffn_weight': _L0_ffn_in['weight'], 'L0_ffn_scale_weight': _L0_ffn_in['scale_weight'], 'L0_ffn_bias': _L0_ffn_in['bias']}

def reference(x, ctx_512, L0_attn_memory, L0_attn_Wq, L0_attn_Wk, L0_attn_Wv, L0_attn_Wo, L0_attn_log_beta, L0_attn_g_state, L0_attn_b_state, L0_attn_g_mem, L0_attn_b_mem, L0_xattn_Wq, L0_xattn_w_kc_q, L0_xattn_w_kc_kv, L0_xattn_W_qr, L0_xattn_W_kr, L0_xattn_Wo, L0_ffn_weight, L0_ffn_scale_weight, L0_ffn_bias):
    import jax
    import jax.numpy as jnp

    def _L0_attn_ref(hidden, memory, Wq, Wk, Wv, Wo, log_beta, g_state, b_state, g_mem, b_mem):
        import jax, jax.numpy as jnp
        import numpy as np
        NUM_STEPS = 3
        NUM_HEADS = 8
        HEAD_DIM = 128
        EPS = 1e-05

        def layernorm(x, g, b):
            mu = jnp.mean(x, -1, keepdims=True)
            var = jnp.mean(jnp.square(x - mu), -1, keepdims=True)
            return (x - mu) * jax.lax.rsqrt(var + EPS) * g + b

        def entmax15(x):
            x = (x - jnp.max(x, -1, keepdims=True)) / 2.0
            xs = jnp.flip(jnp.sort(x, -1), -1)
            rho = jnp.arange(1, x.shape[-1] + 1, dtype=x.dtype)
            mean = jnp.cumsum(xs, -1) / rho
            meansq = jnp.cumsum(xs * xs, -1) / rho
            ss = rho * (meansq - jnp.square(mean))
            tau = mean - jnp.sqrt(jnp.clip((1.0 - ss) / rho, 0.0, None))
            support = jnp.sum(tau <= xs, -1, keepdims=True)
            tau_star = jnp.take_along_axis(tau, support - 1, -1)
            return jnp.square(jnp.clip(x - tau_star, 0.0, None))
        B, S, _ = hidden.shape
        N = memory.shape[0]
        H, hd = (NUM_HEADS, HEAD_DIM)
        Q = layernorm(hidden, g_state, b_state) @ Wq.T
        mn = layernorm(memory, g_mem, b_mem)
        K = (mn @ Wk.T).reshape(N, H, hd).transpose(1, 0, 2)
        V = (mn @ Wv.T).reshape(N, H, hd).transpose(1, 0, 2)
        xi = Q.reshape(B, S, H, hd).transpose(0, 2, 1, 3)
        beta = jnp.exp(log_beta)[None, :, None, None]
        for _ in range(NUM_STEPS):
            scores = jnp.einsum('bhsd,hnd->bhsn', xi, K) * beta
            w = entmax15(scores)
            xi = jnp.einsum('bhsn,hnd->bhsd', w, V)
        out = xi.transpose(0, 2, 1, 3).reshape(B, S, H * hd) @ Wo.T
        return out

    def _L0_xattn_ref(hidden_q, kv_c, Wq, w_kc_q, w_kc_kv, W_qr, W_kr, Wo):
        import jax, jax.numpy as jnp
        import numpy as np
        B, S, L = (2, 128, 128)
        DIM_Q, H, K, D_C, D_CQ, R = (256, 16, 128, 64, 192, 64)

        def _rope_tables(seq_len, dim, dtype):
            inv_freq = 1.0 / 10000.0 ** (jnp.arange(0, dim, 2, dtype=dtype) / dim)
            t = jnp.arange(seq_len, dtype=dtype)
            freqs = t[:, None] * inv_freq[None, :]
            sin = jnp.repeat(jnp.sin(freqs), 2, axis=-1)
            cos = jnp.repeat(jnp.cos(freqs), 2, axis=-1)
            return (sin, cos)

        def _rotate_half(x):
            h = x.shape[-1] // 2
            return jnp.concatenate([-x[..., h:], x[..., :h]], axis=-1)
        b, s, _ = hidden_q.shape
        l = kv_c.shape[1]
        q_hk = (hidden_q @ Wq.T).reshape(b, s, H, K)
        q_big = jnp.einsum('bshk,hkq->bshq', q_hk, w_kc_q)
        sin, cos = _rope_tables(l, D_C, kv_c.dtype)
        kv_rope = kv_c * cos[None] + _rotate_half(kv_c) * sin[None]
        q_r = jnp.einsum('bshq,hqr->bhsr', q_big, W_qr)
        k_r = jnp.einsum('bld,hdr->bhlr', kv_rope, W_kr)
        scores = jnp.einsum('bhsr,bhlr->bhsl', q_r, k_r)
        attn = jax.nn.softmax(scores, axis=-1)
        ctx_c = jnp.einsum('bhsl,bld->bhsd', attn, kv_rope)
        ctx_lat = jnp.einsum('bhsd,hkd->bshk', ctx_c, w_kc_kv)
        out = ctx_lat.reshape(b, s, H * K) @ Wo.T
        return out

    def _L0_ffn_ref(x, weight, scale_weight, bias):
        import jax, jax.numpy as jnp
        import numpy as np
        w = weight * scale_weight[:, None]
        out = jnp.einsum('bsi,oi->bso', x, w) + bias
        return out
    x = _layernorm(x + _L0_attn_ref(x, L0_attn_memory, L0_attn_Wq, L0_attn_Wk, L0_attn_Wv, L0_attn_Wo, L0_attn_log_beta, L0_attn_g_state, L0_attn_b_state, L0_attn_g_mem, L0_attn_b_mem), axis=-1)
    x = _layernorm(x + _L0_xattn_ref(x, ctx_512, L0_xattn_Wq, L0_xattn_w_kc_q, L0_xattn_w_kc_kv, L0_xattn_W_qr, L0_xattn_W_kr, L0_xattn_Wo), axis=-1)
    x = _layernorm(x + _L0_ffn_ref(x, L0_ffn_weight, L0_ffn_scale_weight, L0_ffn_bias), axis=-1)
    return x

_drawn_inputs = setup_inputs


def setup_inputs(seed=0):
    import zlib

    import numpy as np

    out = dict(_drawn_inputs(seed))
    spreads = {'L0_attn_log_beta': (-2.4260151386260986, 0.2),
     'L0_attn_g_state': (1.0, 0.2),
     'L0_attn_b_state': (0.0, 0.1),
     'L0_attn_g_mem': (1.0, 0.2),
     'L0_attn_b_mem': (0.0, 0.1)}
    factors = {'L0_ffn_bias': 3.264}
    for name, (base, spread) in spreads.items():
        noise = np.random.default_rng([zlib.crc32(name.encode()), seed]).standard_normal(out[name].shape)
        drawn = base * np.exp(spread * noise) if base else spread * noise
        out[name] = jnp.asarray(drawn.astype(out[name].dtype))
    for name, factor in factors.items():
        out[name] = (out[name] * factor).astype(out[name].dtype)
    return out
```

```python
from contextlib import ExitStack

import concourse.bass as bass
from concourse import mybir

P = 128
F32 = mybir.dt.float32
ALU = mybir.AluOpType
ACT = mybir.ActivationFunctionType
AX_X = mybir.AxisListType.X
EPS = 1e-5

BATCH, SEQ, HID = 32, 64, 256
ROWS = BATCH * SEQ
TILES = ROWS // P
SLOTS = 2
ITERS = TILES // SLOTS
CT = HID // P
HEADS, SLOTS_MEM = 8, 256
NT = SLOTS_MEM // P
STEPS = 3
EVALS = 6
XH, XD, XQ, XR = 16, 64, 192, 64
PAIRS = XH // 2
N_SMALL = 9
QS = XQ // 2


def memory_stage_order():
    step_len = 4 * (EVALS + 2)
    lag = 2 + 4 * ((EVALS + 2) // 2)
    one = [(-4, "norm_in", 0, 0), (-3, "turn_in", 0, 0)]
    for s in range(STEPS):
        at = s * step_len
        one += [(at, "scores", s, 0), (at + 1, "row_max", s, 0)]
        for e in range(EVALS):
            b = at + 4 + 4 * e
            one += [(b, "resid_lo", s, e), (b + 1, "resid_hi", s, e), (b + 1.2, "square_sum", s, e),
                    (b + 2.5, "root", s, e), (b + 2.6, "newton", s, e)]
        b = at + 4 + 4 * EVALS
        one += [(b, "weights", s, 0), (b + 1, "turn_weights", s, 0), (b + 2, "square_weights", s, 0)]
    b = STEPS * step_len
    one += [(b, "project", 0, 0), (b + 1, "norm_out", 0, 0)]
    both = [(pos + j * lag, j, st, s, e) for j in range(SLOTS) for pos, st, s, e in one]
    return sorted(both, key=lambda r: (r[0], r[1]))


def latent_stage_order():
    one = ["fetch", "turn_x", "queries", "scores", "softmax", "turn_probs", "contexts", "project", "residual"]
    both = [(2 * k + 9 * j, j, st) for j in range(SLOTS) for k, st in enumerate(one)]
    return sorted(both, key=lambda r: (r[0], r[1]))


def ffn_stage_order():
    one = ["norm_in", "turn", "dense", "norm_out"]
    return [(k, j, st) for k, st in enumerate(one) for j in range(SLOTS)]


def prep_jobs():
    jobs = [("mem_t", 0)]
    jobs += [("wk_t", i) for i in range(2)] + [("wv_t", i) for i in range(2)]
    jobs += [("k_t", i) for i in range(4)] + [("v_t", i) for i in range(4)]
    jobs += [("wo_t", i) for i in range(4)]
    jobs += [("score_in", h) for h in range(HEADS)]
    jobs += [("score_step", h) for h in range(HEADS)]
    jobs += [("value_out", h) for h in range(HEADS)]
    jobs += [("wqr_t", i) for i in range(6)] + [("wkr_t", i) for i in range(2)]
    jobs += [("g", i) for i in range(4)]
    jobs += [("xwo_t", i) for i in range(8)]
    for i in range(4):
        jobs += [("j", 4 * i + k) for k in range(4)] + [("a", i)]
    jobs += [("b", i) for i in range(4)] + [("ffn_t", 0)]
    return jobs


def decoder_kernel(nc, x, ctx_kv, memory, Wq, Wk, Wv, Wo, log_beta, g_state, b_state, g_mem, b_mem,
                   xWq, w_kc_q, w_kc_kv, W_qr, W_kr, xWo, ffn_w, ffn_scale, ffn_bias,
                   rope_cos, rope_sin, out):
    jobs = prep_jobs()
    job_no = {job: n for n, job in enumerate(jobs)}
    order_a = memory_stage_order()
    order_b = latent_stage_order()
    order_c = ffn_stage_order()

    x_use = {(j, s): n for n, (j, s) in enumerate([(j, s) for _, j, st, s, _ in order_a if st == "scores"])}
    t_use = {key: n for n, key in enumerate([(j, st, s) for _, j, st, s, _ in order_a
                                             if st in ("turn_in", "turn_weights", "project")])}
    X_USES, T_USES = len(x_use), len(t_use)

    with ExitStack() as ctx:
        def sb(name, shape):
            return ctx.enter_context(nc.sbuf_tensor(name, shape, F32))

        def sem(name):
            return ctx.enter_context(nc.semaphore(name))

        rows = sb("rows", [P, TILES * HID])
        score_in_w = sb("score_in_w", [P, HEADS, CT, SLOTS_MEM])
        score_step_w = sb("score_step_w", [P, HEADS, NT, SLOTS_MEM])
        value_out_w = sb("value_out_w", [P, HEADS, NT, HID])
        latent_q_w = sb("latent_q_w", [P, CT, XH * XD])
        latent_o_w = sb("latent_o_w", [P, PAIRS, HID])
        ffn_wt = sb("ffn_wt", [P, CT, HID])
        ident = sb("ident", [P, P])
        ones_row = sb("ones_row", [1, P])
        bias_row = sb("bias_row", [1, HID])
        beta = sb("beta", [P, HEADS])
        g_col, b_col = sb("g_col", [P, CT]), sb("b_col", [P, CT])
        gm_col, bm_col = sb("gm_col", [P, 1]), sb("bm_col", [P, 1])
        ffn_s = sb("ffn_s", [P, CT])
        cos_sb, sin_sb = sb("cos_sb", [P, 2, XD]), sb("sin_sb", [P, 2, XD])
        stats = sb("stats", [P, SLOTS, 6])
        mean_var = sb("mean_var", [P, SLOTS, 2])
        var_eps, std, rstd = sb("var_eps", [P, SLOTS]), sb("std", [P, SLOTS]), sb("rstd", [P, SLOTS])
        tile_stats = sb("tile_stats", [P, TILES, 6])
        tile_mv = sb("tile_mv", [P, TILES, 2])
        tile_var, tile_std, tile_rstd = sb("tile_var", [P, TILES]), sb("tile_std", [P, TILES]), sb("tile_rstd", [P, TILES])
        small = {n: sb(n, [P, SLOTS, HEADS]) for n in
                 ("neg_max", "one_less_max", "resid_sum", "sq_sum", "sq_root", "inv_sum", "gap", "delta", "neg_tau")}

        region_w = sb("region_w", [P, 14336])
        region_v = sb("region_v", [P, 12288])

        def carve(region, at, *dims):
            n = 1
            for d in dims:
                n *= d
            view = region[:, at:at + n]
            names = "abcd"[:len(dims)]
            if len(dims) == 1:
                return view
            pat = f"p ({' '.join(names)}) -> p {' '.join(names)}"
            return view.rearrange(pat, **{k: d for k, d in zip(names[1:], dims[1:])})

        mem_raw = carve(region_w, 0, NT, P)
        mem_hat = carve(region_w, 256, NT, P)
        mem_t = carve(region_w, 512, SLOTS_MEM)
        wk_raw = carve(region_w, 1024, HEADS, P)
        wv_raw = carve(region_w, 2048, HEADS, P)
        wq_raw = carve(region_w, 3072, HEADS, HID)
        wo_raw = carve(region_w, 5120, CT, HEADS * P)
        wk_t = carve(region_w, 7168, HEADS * P)
        wv_t = carve(region_w, 8192, HEADS * P)
        k_t = carve(region_w, 9216, HEADS, SLOTS_MEM)
        v_t = carve(region_w, 11264, HEADS, SLOTS_MEM)
        wo_t = carve(region_v, 8192, HEADS, HID)

        xwq_raw = carve(region_w, 0, XH, HID)
        kcq_raw = carve(region_w, 4096, XH, XQ)
        kckv_pad = carve(region_w, 7168, XH, P)
        xwo_raw = carve(region_w, 9216, CT, XH * P)
        ffn_raw = carve(region_w, 13312, CT, HID)
        ffn_scaled = carve(region_w, 13824, CT, HID)

        xwo_t = carve(region_v, 0, XH, HID)
        wqr_t = carve(region_v, 4096, XH * XQ)
        wkr_t = carve(region_v, 7168, XH * XD)
        g_sb = carve(region_v, 8192, XH, 2, XD)
        j_sb = carve(region_v, 10240, 4, 2 * HID)
        wqr_raw = carve(rows, 0, 24, XR)
        wkr_raw = carve(rows, 1536, 8, XR)

        resid0 = carve(region_v, 0, SLOTS, HEADS, SLOTS_MEM)
        resid = carve(region_v, 4096, SLOTS, HEADS, SLOTS_MEM)
        weights_t = carve(region_v, 8192, SLOTS, HEADS, NT * P)
        x2 = carve(region_w, 0, SLOTS, HID)
        x2_t = carve(region_w, 512, SLOTS, CT, P)
        out_row = carve(region_w, 1536, SLOTS, HID)
        tile_mv_flat = tile_mv[:, :, :].rearrange("p t k -> p (t k)")
        tile_stats_flat = tile_stats[:, :, :].rearrange("p t k -> p (t k)")

        x_hat = carve(region_w, 0, SLOTS, HID)
        x_hat_t = carve(region_w, 512, SLOTS, CT, P)
        y_row = carve(region_w, 1024, SLOTS, HID)
        junk = carve(region_w, 1536, SLOTS, HEADS, HID)

        lat_x = carve(region_w, 2048, SLOTS, HID)
        lat_x_t = carve(region_w, 2560, SLOTS, CT, P)
        kv_in = carve(region_w, 3072, SLOTS, 2, XD)
        kv_cos = carve(region_w, 3328, SLOTS, 2, XD)
        kv_rot = carve(region_w, 3584, SLOTS, 2, XD)
        kv_diag = carve(region_w, 3840, SLOTS, 2, P)
        kv_diag_t = carve(region_w, 4352, SLOTS, 2, P)
        lat_q_t = carve(region_w, 5120, SLOTS, PAIRS, P)
        probs = carve(region_w, 7168, SLOTS, XH, XD)
        probs_t = carve(region_w, 9216, SLOTS, PAIRS, P)
        lat_c_t = carve(region_w, 11264, SLOTS, PAIRS, P)
        row_nmax, row_sum, row_inv = (carve(region_w, 13312 + 32 * k, SLOTS, XH) for k in range(3))

        banks = ctx.enter_context(nc.psum_tensor("banks", [P, 8, 512], F32))

        def pbank(b, n, *dims):
            view = banks[:, b:b + n, :].rearrange("p b n -> p (b n)")
            if not dims:
                return view
            names = "abc"[:len(dims)]
            return view.rearrange(f"p ({' '.join(names)}) -> p {' '.join(names)}",
                                  **{k: d for k, d in zip(names[1:], dims[1:])})

        ps_scores = pbank(0, 4, HEADS, SLOTS_MEM)
        ps_turn = pbank(4, 4, HEADS, NT, P)
        ps_turn_flat = pbank(4, 4)
        pl_q = pbank(0, 2, PAIRS, P)
        pl_s = pbank(2, 2, XH, XD)
        pl_p = pbank(4, 2, PAIRS, P)
        pl_c = pbank(6, 2, PAIRS, P)

        pd_turn = [pbank(4 * j, 1, 4, P)[:, 0:CT, :] for j in range(SLOTS)]
        pd_dense = [pbank(4 * j + 1, 1)[:, 0:HID] for j in range(SLOTS)]

        ld_mem, ld_w1, ld_small, ld_w2, ld_w3, ld_x = (sem(n) for n in
            ("ld_mem", "ld_w1", "ld_small", "ld_w2", "ld_w3", "ld_x"))
        setup = sem("setup")
        attn_prep_done = sem("attn_prep_done")
        prep_filled = sem("prep_filled")
        prep_emptied = [sem("prep_emptied_act"), sem("prep_emptied_dve")]
        prep_chain = sem("prep_chain")
        mem_var, mem_std, mem_ready, beta_ready, pad_ready = (sem(n) for n in
            ("mem_var", "mem_std", "mem_ready", "beta_ready", "pad_ready"))
        dve_step = sem("dve_step")
        pool_step = sem("pool_step")

        def per_slot(name):
            return [sem(f"{name}{j}") for j in range(SLOTS)]

        var_ready, std_ready, hat_ready = per_slot("var_ready"), per_slot("std_ready"), per_slot("hat_ready")
        turned_in, hat_t_ready = per_slot("turned_in"), per_slot("hat_t_ready")
        scores_ready, offset_ready = per_slot("scores_ready"), per_slot("offset_ready")
        resid_ready, sq_ready, inv_ready = per_slot("resid_ready"), per_slot("sq_ready"), per_slot("inv_ready")
        root_ready, tau_ready = per_slot("root_ready"), per_slot("tau_ready")
        weights_ready, weights_turned, weights_t_ready = (per_slot(n) for n in
            ("weights_ready", "weights_turned", "weights_t_ready"))
        proj_ready = per_slot("proj_ready")
        scores_used = sem("scores_used")
        turn_emptied = sem("turn_emptied")
        row_summed, row_stored = per_slot("row_summed"), per_slot("row_stored")
        norm_step, tile_var_ready, tile_std_ready = sem("norm_step"), sem("tile_var_ready"), sem("tile_std_ready")
        ffn_scaled_ready = sem("ffn_scaled_ready")
        (kv_loaded, kv_read, diag_ready, lat_x_ready, l2_turned, queries_ready, l2_scores_ready, nmax_ready,
         exp_ready, sum_ready, inv_row_ready, probs_ready, probs_turned, contexts_ready, l2_proj_ready) = (per_slot(n) for n in (
            "kv_loaded", "kv_read", "diag_ready", "lat_x_ready", "l2_turned", "queries_ready", "l2_scores_ready",
            "nmax_ready", "exp_ready", "sum_ready", "inv_row_ready", "probs_ready", "probs_turned", "contexts_ready",
            "l2_proj_ready"))
        diag_zero, q_bank_free, p_bank_free, c_bank_free, scores_shifted = (sem(n) for n in
            ("diag_zero", "q_bank_free", "p_bank_free", "c_bank_free", "scores_shifted"))
        x2_ready, l3_turned, x2_t_ready, dense_ready, dense_read, out_ready, stored = (per_slot(n) for n in
            ("x2_ready", "l3_turned", "x2_t_ready", "dense_ready", "dense_read", "out_ready", "stored"))


        with nc.Block() as block:
            @block.sync
            def _(sp):
                sp.dma_start(mem_raw, memory.rearrange("(t p) c -> p t c", p=P)).then_inc(ld_mem, 16)
                sp.dma_start(wk_raw, Wk.rearrange("(h p) c -> p h c", p=P)).then_inc(ld_w1, 16)
                sp.dma_start(wv_raw, Wv.rearrange("(h p) c -> p h c", p=P)).then_inc(ld_w1, 16)
                sp.dma_start(wo_raw, Wo.rearrange("(t p) c -> p t c", p=P)).then_inc(ld_w1, 16)
                sp.dma_start(wq_raw, Wq.rearrange("(h p) c -> p h c", p=P)).then_inc(ld_w1, 16)
                sp.dma_start(wqr_raw, W_qr.rearrange("h q r -> (h q) r").rearrange("(t p) r -> p t r", p=P)).then_inc(ld_w2, 16)
                sp.dma_start(wkr_raw, W_kr.rearrange("h d r -> (h d) r").rearrange("(t p) r -> p t r", p=P)).then_inc(ld_w2, 16)
                n_attn = job_no[("value_out", HEADS - 1)] + 1
                sp.wait_ge(prep_emptied[0], (n_attn + 1) // 2)
                sp.wait_ge(prep_emptied[1], n_attn // 2)
                sp.dma_start(xwo_raw, xWo.rearrange("(t p) c -> p t c", p=P)).then_inc(ld_w3, 16)
                sp.dma_start(xwq_raw, xWq.rearrange("(h p) c -> p h c", p=P)).then_inc(ld_w3, 16)
                sp.dma_start(kcq_raw, w_kc_q.rearrange("h k q -> k h q")).then_inc(ld_w3, 16)
                sp.dma_start(ffn_raw, ffn_w.rearrange("(t p) c -> p t c", p=P)).then_inc(ld_w3, 16)
                sp.wait_ge(pad_ready, 1)
                kp = kckv_pad.rearrange("p (g two) d -> p g two d", two=2)
                src = w_kc_kv.rearrange("(g two) k d -> k g two d", two=2)
                for odd in range(2):
                    sp.dma_start(kp[:, :, odd, odd * XD:(odd + 1) * XD], src[:, :, odd, :]).then_inc(ld_w3, 16)
                n_turned = job_no[("wkr_t", 1)] + 1
                sp.wait_ge(prep_emptied[0], (n_turned + 1) // 2)
                sp.wait_ge(prep_emptied[1], n_turned // 2)
                sp.dma_start(rows[:, :].rearrange("p (t c) -> p t c", c=HID),
                             x.rearrange("(t p) c -> p t c", p=P)).then_inc(ld_x, 16)
                sp.wait_ge(ld_x, 16)

            @block.gpsimd
            def _(pool):
                pool.dma_start(beta[:, :], log_beta.rearrange("(a h) -> a h", a=1).to_broadcast([P, HEADS])).then_inc(ld_small, 16)
                for col, src in ((g_col, g_state), (b_col, b_state), (gm_col, g_mem), (bm_col, b_mem), (ffn_s, ffn_scale)):
                    pool.dma_start(col[:, :], src.rearrange("(t p) -> p t", p=P),
                                   allow_slow_non_contiguous=True).then_inc(ld_small, 16)
                pool.dma_start(bias_row[:, :], ffn_bias.rearrange("(a n) -> a n", a=1)).then_inc(ld_small, 16)
                pool.dma_start(cos_sb[:, :, :], rope_cos.rearrange("p (b d) -> p b d", b=2)).then_inc(ld_small, 16)
                pool.dma_start(sin_sb[:, :, :], rope_sin.rearrange("p (b d) -> p b d", b=2)).then_inc(ld_small, 16)
                nc.gpsimd.memset(ident[:, :], 0.0).then_inc(setup, 1)
                nc.gpsimd.memset(ones_row[:, :], 1.0).then_inc(setup, 1)
                pool.wait_ge(setup, 2)
                nc.gpsimd.affine_select(out=ident[:, :], in_=ident[:, :], compare_op=ALU.not_equal, fill=1.0, base=0,
                                        pattern=[[-1, P]], channel_multiplier=1).then_inc(setup, 1)
                n_attn = job_no[("value_out", HEADS - 1)] + 1
                pool.wait_ge(prep_emptied[0], (n_attn + 1) // 2)
                pool.wait_ge(prep_emptied[1], n_attn // 2)
                nc.gpsimd.memset(kckv_pad, 0.0).then_inc(pad_ready, 1)
                pool.wait_ge(ld_small, 16 * N_SMALL)

            def evacuate(eng, which):
                def copy(dst, src):
                    if which == 0:
                        return nc.scalar.activation(dst, src, ACT.Copy)
                    return nc.vector.tensor_copy(dst, src)

                def scaled(dst, src, col):
                    if which == 0:
                        return nc.scalar.activation(dst, src, ACT.Copy, scale=col)
                    return nc.vector.tensor_scalar(dst, src, col, None, ALU.mult)

                for n, (kind, i) in enumerate(jobs):
                    if n % 2 != which:
                        continue
                    eng.wait_ge(prep_filled, n + 1)
                    bank = banks[:, n % 8, :]
                    half = bank.rearrange("p (a b) -> p a b", a=2)
                    if kind == "mem_t":
                        eng.wait_ge(ld_small, 16 * N_SMALL)
                        ins = nc.scalar.activation(mem_t, bank[:, 0:SLOTS_MEM], ACT.Identity,
                                                   scale=gm_col[:, 0:1], bias=bm_col[:, 0:1])
                    elif kind == "wk_t":
                        ins = copy(wk_t[:, 512 * i:512 * (i + 1)], bank)
                    elif kind == "wv_t":
                        ins = copy(wv_t[:, 512 * i:512 * (i + 1)], bank)
                    elif kind == "k_t":
                        ins = copy(k_t[:, 2 * i:2 * i + 2, :], half)
                    elif kind == "v_t":
                        ins = copy(v_t[:, 2 * i:2 * i + 2, :], half)
                    elif kind == "wo_t":
                        ins = copy(wo_t[:, 2 * i:2 * i + 2, :], half)
                    elif kind == "score_in":
                        if i < 2:
                            eng.wait_ge(beta_ready, 2)
                        ins = scaled(score_in_w[:, i, :, :], half, beta[:, i:i + 1])
                    elif kind == "score_step":
                        ins = scaled(score_step_w[:, i, :, :], half, beta[:, i:i + 1])
                    elif kind == "value_out":
                        ins = copy(value_out_w[:, i, :, :], half)
                    elif kind == "wqr_t":
                        ins = copy(wqr_t[0:XR, 512 * i:512 * (i + 1)], bank[0:XR, :])
                    elif kind == "wkr_t":
                        ins = copy(wkr_t[0:XR, 512 * i:512 * (i + 1)], bank[0:XR, :])
                    elif kind == "g":
                        ins = copy(g_sb[0:QS, 4 * i:4 * i + 4, :, :],
                                   bank[0:QS, :].rearrange("p (h t d) -> p h t d", h=4, t=2))
                    elif kind == "xwo_t":
                        if which == 1 and i in (0, 1):
                            eng.wait_ge(ld_w3, 16 * 6)
                            for t in range(CT):
                                nc.vector.tensor_scalar(ffn_scaled[:, t, :], ffn_raw[:, t, :], ffn_s[:, t:t + 1], None,
                                                        ALU.mult).then_inc(ffn_scaled_ready, 1)
                        ins = copy(xwo_t[:, 2 * i:2 * i + 2, :], half)
                    elif kind == "j":
                        ins = copy(j_sb[0:QS, i % 4, :], bank[0:QS, :])
                    elif kind == "a":
                        ins = copy(latent_q_w[:, :, 4 * XD * i:4 * XD * (i + 1)], half)
                    elif kind == "b":
                        ins = copy(latent_o_w[:, 2 * i:2 * i + 2, :], half)
                    elif kind == "ffn_t":
                        ins = copy(ffn_wt[:, :, :], half)
                    ins.then_inc(prep_emptied[which], 1)

            @block.scalar
            def _(act):
                act.wait_ge(mem_var, 1)
                nc.scalar.activation(std[:, 0:NT], var_eps[:, 0:NT], ACT.Sqrt).then_inc(mem_std, 1)
                act.wait_ge(ld_small, 16 * N_SMALL)
                nc.scalar.activation(beta[:, :], beta[:, :], ACT.Exp).then_inc(beta_ready, 1)
                act.wait_ge(beta_ready, 1)
                nc.scalar.activation(beta[:, :], beta[:, :], ACT.Copy, scale=0.5).then_inc(beta_ready, 1)
                evacuate(act, 0)

            @block.vector
            def _(dve):
                dve.wait_ge(ld_mem, 16)
                for t in range(NT):
                    nc.vector.bn_stats(stats[:, t, :], mem_raw[:, t, :]).then_inc(prep_chain, 1)
                dve.wait_ge(prep_chain, NT)
                for t in range(NT):
                    nc.vector.bn_aggr(mean_var[:, t, :], stats[:, t, :]).then_inc(prep_chain, 1)
                dve.wait_ge(prep_chain, 2 * NT)
                nc.vector.tensor_scalar(var_eps[:, 0:NT], mean_var[:, 0:NT, 1], EPS, None, ALU.add).then_inc(mem_var, 1)
                dve.wait_ge(mem_std, 1)
                nc.vector.reciprocal(rstd[:, 0:NT], std[:, 0:NT]).then_inc(prep_chain, 1)
                dve.wait_ge(prep_chain, 2 * NT + 1)
                for t in range(NT):
                    nc.vector.tensor_scalar(mem_hat[:, t, :], mem_raw[:, t, :], mean_var[:, t, 0:1], rstd[:, t:t + 1],
                                            ALU.subtract, ALU.mult).then_inc(mem_ready, 1)
                dve.wait_ge(beta_ready, 2)
                dve.wait_ge(ld_small, 16 * N_SMALL)
                evacuate(dve, 1)
                dve.wait_ge(ld_x, 16)
                for t in range(TILES):
                    nc.vector.bn_stats(tile_stats[:, t, :], rows[:, HID * t:HID * (t + 1)])

            @block.tensor
            def _(pe):
                def emptied(kind, i):
                    n = job_no[(kind, i)] + 1
                    pe.wait_ge(prep_emptied[0], (n + 1) // 2)
                    if n // 2:
                        pe.wait_ge(prep_emptied[1], n // 2)

                pe.wait_ge(setup, 3)
                for n, (kind, i) in enumerate(jobs):
                    if n >= 8:
                        pe.wait_ge(prep_emptied[n % 2], (n - 8) // 2 + 1)
                    bank = banks[:, n % 8, :]
                    mm = []
                    T = nc.tensor.transpose

                    def M(out, lhsT, rhs, start, stop):
                        return nc.tensor.matmul(out, lhsT, rhs, start=start, stop=stop)

                    if kind == "mem_t":
                        pe.wait_ge(mem_ready, NT)
                        for t in range(NT):
                            ins = T(bank[:, P * t:P * (t + 1)], mem_hat[:, t, :], ident[:, :])
                    elif kind in ("wk_t", "wv_t"):
                        pe.wait_ge(ld_w1, 64)
                        raw = wk_raw if kind == "wk_t" else wv_raw
                        for q in range(4):
                            ins = T(bank[:, P * q:P * (q + 1)], raw[:, 4 * i + q, :], ident[:, :])
                    elif kind in ("k_t", "v_t"):
                        emptied("wv_t", 1)
                        w = wk_t if kind == "k_t" else wv_t
                        for q in range(2):
                            h = 2 * i + q
                            ins = M(bank[:, 256 * q:256 * (q + 1)], w[:, P * h:P * (h + 1)], mem_t, True, True)
                    elif kind == "wo_t":
                        for q in range(2):
                            h = 2 * i + q
                            for t in range(CT):
                                ins = T(bank[:, 256 * q + P * t:256 * q + P * (t + 1)],
                                        wo_raw[:, t, P * h:P * (h + 1)], ident[:, :])
                    elif kind == "score_in":
                        emptied("v_t", 3)
                        for t in range(CT):
                            ins = M(bank[:, 256 * t:256 * (t + 1)], wq_raw[:, i, P * t:P * (t + 1)], k_t[:, i, :], True, True)
                    elif kind == "score_step":
                        for t in range(NT):
                            ins = M(bank[:, 256 * t:256 * (t + 1)], v_t[:, i, P * t:P * (t + 1)], k_t[:, i, :], True, True)
                    elif kind == "value_out":
                        emptied("wo_t", 3)
                        for t in range(NT):
                            ins = M(bank[:, 256 * t:256 * (t + 1)], v_t[:, i, P * t:P * (t + 1)], wo_t[:, i, :], True, True)
                    elif kind == "wqr_t":
                        pe.wait_ge(ld_w2, 32)
                        for q in range(4):
                            ins = T(bank[0:XR, P * q:P * (q + 1)], wqr_raw[:, 4 * i + q, :], ident[:, :])
                    elif kind == "wkr_t":
                        for q in range(4):
                            ins = T(bank[0:XR, P * q:P * (q + 1)], wkr_raw[:, 4 * i + q, :], ident[:, :])
                    elif kind == "g":
                        emptied("wkr_t", 1)
                        for q in range(4):
                            h = 4 * i + q
                            for t in range(2):
                                ins = M(bank[0:QS, P * q + XD * t:P * q + XD * (t + 1)],
                                        wqr_t[0:XR, XQ * h + QS * t:XQ * h + QS * (t + 1)],
                                        wkr_t[0:XR, XD * h:XD * (h + 1)], True, True)
                    elif kind == "xwo_t":
                        pe.wait_ge(ld_w3, 16 * 6)
                        for q in range(2):
                            h = 2 * i + q
                            for t in range(CT):
                                ins = T(bank[:, 256 * q + P * t:256 * q + P * (t + 1)],
                                        xwo_raw[:, t, P * h:P * (h + 1)], ident[:, :])
                    elif kind == "j":
                        if i >= 4:
                            emptied("a", i // 4 - 1)
                        for t in range(2):
                            ins = M(bank[0:QS, 256 * t:256 * (t + 1)], kcq_raw[:, i, QS * t:QS * (t + 1)],
                                    xwq_raw[:, i, :], True, True)
                    elif kind == "a":
                        emptied("j", 4 * i + 3)
                        for c in range(CT):
                            for q in range(4):
                                h = 4 * i + q
                                for t in range(2):
                                    ins = M(bank[:, 256 * c + XD * q:256 * c + XD * (q + 1)],
                                            j_sb[0:QS, h % 4, 256 * t + P * c:256 * t + P * (c + 1)],
                                            g_sb[0:QS, h, t, :], t == 0, t == 1)
                    elif kind == "b":
                        emptied("xwo_t", 7)
                        for q in range(2):
                            g = 2 * i + q
                            for odd in range(2):
                                ins = M(bank[:, 256 * q:256 * (q + 1)], kckv_pad[:, 2 * g + odd, :],
                                        xwo_t[:, 2 * g + odd, :], odd == 0, odd == 1)
                    elif kind == "ffn_t":
                        pe.wait_ge(ffn_scaled_ready, CT)
                        for c in range(CT):
                            for t in range(CT):
                                ins = T(bank[:, 256 * c + P * t:256 * c + P * (t + 1)],
                                        ffn_scaled[:, t, P * c:P * (c + 1)], ident[:, :])
                    ins.then_inc(prep_filled, 1)

        X_EACH, T_EACH = HEADS, 4

        def x_used(it, j, s, n):
            return it * (X_USES * X_EACH) + (x_use[(j, s)] * X_EACH + n)

        def t_emptied(it, key, n):
            return it * (T_USES * T_EACH) + (t_use[key] * T_EACH + n)

        def count(it, per, n):
            return it * per + n

        def row_norms(dve, layer):
            base = 3 * layer
            for t in range(TILES):
                ins = nc.vector.bn_aggr(tile_mv[:, t, :], tile_stats[:, t, :])
            ins.then_inc(norm_step, 1)
            dve.wait_ge(norm_step, base + 1)
            nc.vector.tensor_scalar(tile_var[:, :], tile_mv[:, :, 1], EPS, None, ALU.add).then_inc(tile_var_ready, 1)
            dve.wait_ge(tile_std_ready, layer + 1)
            nc.vector.reciprocal(tile_rstd[:, :], tile_std[:, :]).then_inc(norm_step, 2)
            dve.wait_ge(norm_step, base + 3)

        def row_roots(act, layer):
            act.wait_ge(tile_var_ready, layer + 1)
            nc.scalar.activation(tile_std[:, :], tile_var[:, :], ACT.Sqrt).then_inc(tile_std_ready, 1)

        def tile_mean(tile):
            return tile_mv_flat[:, bass.ds(tile * 2, 1)]

        def store_row(pool, it_total, j, it):
            pool.wait_ge(row_summed[j], count(it_total, 1, 1))
            tile = it * SLOTS + j
            nc.gpsimd.tensor_copy(rows[:, bass.ds(tile * HID, HID)], y_row[:, j, :]).then_inc(row_stored[j], 1)
            nc.gpsimd.tensor_copy(tile_stats_flat[:, bass.ds(tile * 6, 6)], stats[:, j, :]).then_inc(row_stored[j], 1)

        with nc.Block() as block:
            @block.scalar
            def _(act):
                row_roots(act, 0)
                with act.Fori(0, ITERS) as it:
                    for _, j, stage, s, e in order_a:
                        ev = s * EVALS + e
                        if stage == "turn_in":
                            act.wait_ge(turned_in[j], count(it, 1, 1))
                            for t in range(CT):
                                nc.scalar.activation(x_hat_t[:, j, t, :], ps_turn_flat[:, P * t:P * (t + 1)], ACT.Identity,
                                                     scale=g_col[:, t:t + 1], bias=b_col[:, t:t + 1]).then_inc(turn_emptied, 2)
                        elif stage in ("resid_lo", "resid_hi"):
                            half = range(0, 4) if stage == "resid_lo" else range(4, HEADS)
                            if e == 0:
                                act.wait_ge(offset_ready[j], count(it, STEPS, s + 1))
                                for h in half:
                                    nc.scalar.activation(resid0[:, j, h, :], ps_scores[:, h, :], ACT.Relu,
                                                         bias=small["one_less_max"][:, j, h:h + 1],
                                                         accum_out=small["resid_sum"][:, j, h:h + 1]).then_inc(scores_used, 1)
                            else:
                                act.wait_ge(tau_ready[j], count(it, STEPS * EVALS, ev))
                                for h in half:
                                    nc.scalar.activation(resid[:, j, h, :], resid0[:, j, h, :], ACT.Relu,
                                                         bias=small["neg_tau"][:, j, h:h + 1],
                                                         accum_out=small["resid_sum"][:, j, h:h + 1]).then_inc(resid_ready[j], 1)
                        elif stage == "root":
                            act.wait_ge(sq_ready[j], count(it, STEPS * EVALS, ev + 1))
                            nc.scalar.activation(small["sq_root"][:, j, :], small["sq_sum"][:, j, :],
                                                 ACT.Sqrt).then_inc(root_ready[j], 1)
                        elif stage == "square_weights":
                            for q in range(4):
                                act.wait_ge(weights_turned[j], count(it, STEPS * 4, s * 4 + q + 1))
                                nc.scalar.activation(weights_t[:, j, 2 * q:2 * q + 2, :], ps_turn_flat[:, 512 * q:512 * (q + 1)]
                                                     .rearrange("p (h n) -> p h n", h=2), ACT.Square).then_inc(turn_emptied, 1)

            @block.vector
            def _(dve):
                per = SLOTS * STEPS
                row_norms(dve, 0)
                with dve.Fori(0, ITERS) as it:
                    n_step = 0
                    for _, j, stage, s, e in order_a:
                        ev = s * EVALS + e
                        row_tile = rows[:, bass.ds((it * SLOTS + j) * HID, HID)]
                        if stage == "norm_in":
                            nc.vector.tensor_scalar(x_hat[:, j, :], row_tile, tile_mean(it * SLOTS + j),
                                                    tile_rstd[:, bass.ds(it * SLOTS + j, 1)],
                                                    ALU.subtract, ALU.mult).then_inc(hat_ready[j], 1)
                        elif stage == "row_max":
                            for q in range(4):
                                dve.wait_ge(scores_ready[j], count(it, STEPS * 4, s * 4 + q + 1))
                                ins = nc.vector.tensor_reduce(small["neg_max"][:, j, 2 * q:2 * q + 2],
                                                              ps_scores[:, 2 * q:2 * q + 2, :], AX_X, ALU.max, negate=True)
                            ins.then_inc(dve_step, 1)
                            n_step += 1
                            dve.wait_ge(dve_step, count(it, per, n_step))
                            nc.vector.tensor_scalar(small["one_less_max"][:, j, :], small["neg_max"][:, j, :], 1.0, None,
                                                    ALU.add).then_inc(offset_ready[j], 1)
                        elif stage == "square_sum":
                            for h in range(HEADS):
                                if e == 0:
                                    dve.wait_ge(scores_used, x_used(it, j, s, h + 1))
                                    r = resid0[:, j, h, :]
                                else:
                                    dve.wait_ge(resid_ready[j], count(it, STEPS * (EVALS - 1) * HEADS,
                                                                      (s * (EVALS - 1) + e - 1) * HEADS + h + 1))
                                    r = resid[:, j, h, :]
                                ins = nc.vector.scalar_tensor_tensor(out=junk[:, j, h, :], in0=r, scalar=1.0, in1=r, op0=ALU.mult,
                                                                     op1=ALU.mult, accum_out=small["sq_sum"][:, j, h:h + 1])
                            ins.then_inc(sq_ready[j], 1)
                            nc.vector.reciprocal(small["inv_sum"][:, j, :], small["resid_sum"][:, j, :]).then_inc(inv_ready[j], 1)
                        elif stage == "weights":
                            dve.wait_ge(tau_ready[j], count(it, STEPS * EVALS, s * EVALS + EVALS))
                            for h in range(HEADS):
                                ins = nc.vector.tensor_scalar(resid[:, j, h, :], resid0[:, j, h, :],
                                                              small["neg_tau"][:, j, h:h + 1], 0.0, ALU.add, ALU.max)
                                if h % 2:
                                    ins.then_inc(weights_ready[j], 1)
                        elif stage == "norm_out":
                            dve.wait_ge(proj_ready[j], count(it, 1, 1))
                            dve.wait_ge(row_stored[j], count(it, 2, 0))
                            nc.vector.tensor_tensor(y_row[:, j, :], ps_turn_flat[:, 0:HID], row_tile,
                                                    ALU.add).then_inc(turn_emptied, T_EACH)
                            dve.wait_ge(turn_emptied, t_emptied(it, (j, "project", 0), T_EACH))
                            nc.vector.bn_stats(stats[:, j, :], y_row[:, j, :]).then_inc(row_summed[j], 1)
                    assert n_step == per, (n_step, per)

            @block.gpsimd
            def _(pool):
                per = SLOTS * STEPS * (2 * EVALS - 1)
                with pool.Fori(0, ITERS) as it:
                    n_step = 0
                    for _, j, stage, s, e in order_a:
                        if stage == "norm_out":
                            store_row(pool, it, j, it)
                        if stage != "newton":
                            continue
                        v = {k: t[:, j, :] for k, t in small.items()}
                        pool.wait_ge(root_ready[j], count(it, STEPS * EVALS, s * EVALS + e + 1))
                        pool.wait_ge(inv_ready[j], count(it, STEPS * EVALS, s * EVALS + e + 1))
                        nc.gpsimd.tensor_tensor(v["gap"], v["sq_root"], v["sq_sum"], ALU.subtract).then_inc(pool_step, 1)
                        n_step += 1
                        pool.wait_ge(pool_step, count(it, per, n_step))
                        if e == 0:
                            nc.gpsimd.tensor_tensor(v["neg_tau"], v["gap"], v["inv_sum"], ALU.mult).then_inc(tau_ready[j], 1)
                        else:
                            nc.gpsimd.tensor_tensor(v["delta"], v["gap"], v["inv_sum"], ALU.mult).then_inc(pool_step, 1)
                            n_step += 1
                            pool.wait_ge(pool_step, count(it, per, n_step))
                            nc.gpsimd.tensor_tensor(v["neg_tau"], v["neg_tau"], v["delta"], ALU.add).then_inc(tau_ready[j], 1)
                    assert n_step == per

            @block.tensor
            def _(pe):
                with pe.Fori(0, ITERS) as it:
                    for _, j, stage, s, e in order_a:
                        if stage == "turn_in":
                            pe.wait_ge(hat_ready[j], count(it, 1, 1))
                            pe.wait_ge(turn_emptied, t_emptied(it, (j, stage, 0), 0))
                            for t in range(CT):
                                ins = nc.tensor.transpose(ps_turn_flat[:, P * t:P * (t + 1)], x_hat[:, j, P * t:P * (t + 1)],
                                                          ident[:, :])
                            ins.then_inc(turned_in[j], 1)
                        elif stage == "scores":
                            for q in range(4):
                                if s == 0 and q == 0:
                                    pe.wait_ge(turn_emptied, t_emptied(it, (j, "turn_in", 0), T_EACH))
                                if s:
                                    pe.wait_ge(turn_emptied, t_emptied(it, (j, "turn_weights", s - 1), q + 1))
                                pe.wait_ge(scores_used, x_used(it, j, s, 0))
                                for h in (2 * q, 2 * q + 1):
                                    for t in range(CT):
                                        lhsT = x_hat_t[:, j, t, :] if s == 0 else weights_t[:, j, h, P * t:P * (t + 1)]
                                        w = score_in_w if s == 0 else score_step_w
                                        ins = nc.tensor.matmul(ps_scores[:, h, :], lhsT, w[:, h, t, :],
                                                               start=(t == 0), stop=(t == CT - 1))
                                ins.then_inc(scores_ready[j], 1)
                        elif stage == "turn_weights":
                            for q in range(4):
                                pe.wait_ge(weights_ready[j], count(it, STEPS * 4, s * 4 + q + 1))
                                pe.wait_ge(turn_emptied, t_emptied(it, (j, stage, s), 0))
                                for h in (2 * q, 2 * q + 1):
                                    for t in range(NT):
                                        ins = nc.tensor.transpose(ps_turn[:, h, t, :], resid[:, j, h, P * t:P * (t + 1)],
                                                                  ident[:, :])
                                ins.then_inc(weights_turned[j], 1)
                        elif stage == "project":
                            pe.wait_ge(turn_emptied, t_emptied(it, (j, stage, 0), 0))
                            for h in range(HEADS):
                                for t in range(NT):
                                    ins = nc.tensor.matmul(ps_turn_flat[:, 0:HID], weights_t[:, j, h, P * t:P * (t + 1)],
                                                           value_out_w[:, h, t, :], start=(h == 0 and t == 0),
                                                           stop=(h == HEADS - 1 and t == NT - 1))
                            ins.then_inc(proj_ready[j], 1)

        with nc.Block() as block:
            @block.sync
            def _(sp):
                with sp.Fori(0, ITERS) as it:
                    for j in range(SLOTS):
                        sp.wait_ge(kv_read[j], count(it, 1, 0))
                        src = ctx_kv.rearrange("b l d -> l b d")[:, bass.ds((it * SLOTS + j) * 2, 2), :]
                        for half in range(2):
                            sp.dma_start(kv_in[64 * half:64 * (half + 1), j, :, :], src).then_inc(kv_loaded[j], 16)

            @block.gpsimd
            def _(pool):
                nc.gpsimd.memset(kv_diag, 0.0).then_inc(diag_zero, 1)
                pool.wait_ge(diag_zero, 1)
                per = SLOTS * 1
                with pool.Fori(0, ITERS) as it:
                    n_step = 0
                    for _, j, stage in order_b:
                        if stage == "fetch":
                            pool.wait_ge(kv_loaded[j], count(it, 32, 32))
                            H = XD // 2
                            nc.gpsimd.tensor_tensor(kv_cos[:, j, :, :], kv_in[:, j, :, :], cos_sb[:, :, :], ALU.mult)
                            nc.gpsimd.tensor_tensor(kv_rot[:, j, :, 0:H], kv_in[:, j, :, H:XD], sin_sb[:, :, 0:H], ALU.mult)
                            nc.gpsimd.tensor_tensor(kv_rot[:, j, :, H:XD], kv_in[:, j, :, 0:H], sin_sb[:, :, H:XD],
                                                    ALU.mult).then_inc(kv_read[j], 1)
                            pool.wait_ge(kv_read[j], count(it, 1, 1))
                            pool.wait_ge(contexts_ready[j], count(it, 1, 0))
                            for half in range(2):
                                at = slice(64 * half, 64 * (half + 1))
                                nc.gpsimd.tensor_tensor(kv_diag[at, j, :, XD * half:XD * (half + 1)], kv_cos[at, j, :, :],
                                                        kv_rot[at, j, :, :], ALU.add).then_inc(diag_ready[j], 1)
                        elif stage == "softmax":
                            pool.wait_ge(inv_row_ready[j], count(it, 1, 1))
                            nc.gpsimd.tensor_tensor(probs[:, j, :, :], probs[:, j, :, :],
                                                    row_inv[:, j, :].unsqueeze(2).to_broadcast([P, XH, XD]),
                                                    ALU.mult).then_inc(probs_ready[j], 1)
                        elif stage == "residual":
                            store_row(pool, it + ITERS, j, it)

            @block.scalar
            def _(act):
                row_roots(act, 1)
                with act.Fori(0, ITERS) as it:
                    for n, (_, j, stage) in enumerate(order_b):
                        if stage == "turn_x":
                            act.wait_ge(l2_turned[j], count(it, 1, 1))
                            nc.scalar.activation(lat_x_t[:, j, :, :], pl_q[:, 0:2, :], ACT.Copy).then_inc(q_bank_free, 1)
                            nc.scalar.activation(kv_diag_t[:, j, :, :], pl_q[:, 2:4, :], ACT.Copy).then_inc(q_bank_free, 1)
                        elif stage == "queries":
                            for q in range(2):
                                act.wait_ge(queries_ready[j], count(it, 2, q + 1))
                                nc.scalar.activation(lat_q_t[:, j, 4 * q:4 * q + 4, :], pl_q[:, 4 * q:4 * q + 4, :],
                                                     ACT.Copy).then_inc(q_bank_free, 1)
                        elif stage == "softmax":
                            act.wait_ge(scores_shifted, count(it, 2, j + 1))
                            nc.scalar.activation(probs[:, j, :, :], probs[:, j, :, :], ACT.Exp).then_inc(exp_ready[j], 1)
                        elif stage == "turn_probs":
                            for q in range(2):
                                act.wait_ge(probs_turned[j], count(it, 2, q + 1))
                                nc.scalar.activation(probs_t[:, j, 4 * q:4 * q + 4, :], pl_p[:, 4 * q:4 * q + 4, :],
                                                     ACT.Copy).then_inc(p_bank_free, 1)

            @block.vector
            def _(dve):
                row_norms(dve, 1)
                with dve.Fori(0, ITERS) as it:
                    for n, (_, j, stage) in enumerate(order_b):
                        if stage == "fetch":
                            dve.wait_ge(l2_turned[j], count(it, 1, 0))
                            tile = it * SLOTS + j
                            nc.vector.tensor_scalar(lat_x[:, j, :], rows[:, bass.ds(tile * HID, HID)], tile_mean(tile),
                                                    tile_rstd[:, bass.ds(tile, 1)],
                                                    ALU.subtract, ALU.mult).then_inc(lat_x_ready[j], 1)
                        elif stage == "softmax":
                            dve.wait_ge(l2_scores_ready[j], count(it, 1, 1))
                            nc.vector.tensor_reduce(row_nmax[:, j, :], pl_s, AX_X, ALU.max, negate=True).then_inc(nmax_ready[j], 1)
                            dve.wait_ge(nmax_ready[j], count(it, 1, 1))
                            nc.vector.tensor_tensor(probs[:, j, :, :], pl_s,
                                                    row_nmax[:, j, :].unsqueeze(2).to_broadcast([P, XH, XD]),
                                                    ALU.add).then_inc(scores_shifted, 1)
                            dve.wait_ge(exp_ready[j], count(it, 1, 1))
                            nc.vector.tensor_reduce(row_sum[:, j, :], probs[:, j, :, :], AX_X, ALU.add).then_inc(sum_ready[j], 1)
                            dve.wait_ge(sum_ready[j], count(it, 1, 1))
                            nc.vector.reciprocal(row_inv[:, j, :], row_sum[:, j, :]).then_inc(inv_row_ready[j], 1)
                        elif stage == "contexts":
                            dve.wait_ge(contexts_ready[j], count(it, 1, 1))
                            nc.vector.tensor_copy(lat_c_t[:, j, :, :], pl_c).then_inc(c_bank_free, 1)
                        elif stage == "residual":
                            dve.wait_ge(l2_proj_ready[j], count(it, 1, 1))
                            dve.wait_ge(row_stored[j], count(it, 2, 2 * ITERS))
                            nc.vector.tensor_tensor(y_row[:, j, :], pl_c[:, 0:2, :].rearrange("p a b -> p (a b)"),
                                                    lat_x[:, j, :], ALU.add).then_inc(c_bank_free, 1)
                            dve.wait_ge(c_bank_free, count(it, 4, 2 * j + 2))
                            nc.vector.bn_stats(stats[:, j, :], y_row[:, j, :]).then_inc(row_summed[j], 1)

            @block.tensor
            def _(pe):
                q_n = c_n = p_n = 0
                with pe.Fori(0, ITERS) as it:
                    for _, j, stage in order_b:
                        if stage == "turn_x":
                            pe.wait_ge(lat_x_ready[j], count(it, 1, 1))
                            pe.wait_ge(diag_ready[j], count(it, 2, 2))
                            pe.wait_ge(q_bank_free, count(it, 8, q_n))
                            for t in range(CT):
                                nc.tensor.transpose(pl_q[:, t, :], lat_x[:, j, P * t:P * (t + 1)], ident[:, :])
                            for b in range(2):
                                ins = nc.tensor.transpose(pl_q[:, 2 + b, :], kv_diag[:, j, b, :], ident[:, :])
                            ins.then_inc(l2_turned[j], 1)
                            q_n += 2
                        elif stage == "queries":
                            pe.wait_ge(q_bank_free, count(it, 8, q_n))
                            for g in range(PAIRS):
                                for t in range(CT):
                                    ins = nc.tensor.matmul(pl_q[:, g, :], latent_q_w[:, t, P * g:P * (g + 1)],
                                                           lat_x_t[:, j, t, :], start=(t == 0), stop=(t == CT - 1))
                                if g % 4 == 3:
                                    ins.then_inc(queries_ready[j], 1)
                            q_n += 2
                        elif stage == "scores":
                            pe.wait_ge(q_bank_free, count(it, 8, q_n))
                            pe.wait_ge(scores_shifted, count(it, 2, j))
                            for g in range(PAIRS):
                                for b in range(2):
                                    at = slice(64 * b, 64 * (b + 1))
                                    ins = nc.tensor.matmul(pl_s[at, 2 * g:2 * g + 2, :], lat_q_t[:, j, g, at],
                                                           kv_diag_t[:, j, b, :], start=True, stop=True)
                            ins.then_inc(l2_scores_ready[j], 1)
                        elif stage == "turn_probs":
                            pe.wait_ge(probs_ready[j], count(it, 1, 1))
                            pe.wait_ge(p_bank_free, count(it, 4, p_n))
                            for g in range(PAIRS):
                                ins = nc.tensor.transpose(pl_p[:, g, :], probs[:, j, 2 * g:2 * g + 2, :]
                                                          .rearrange("p h l -> p (h l)"), ident[:, :])
                                if g % 4 == 3:
                                    ins.then_inc(probs_turned[j], 1)
                            p_n += 2
                        elif stage == "contexts":
                            pe.wait_ge(p_bank_free, count(it, 4, p_n))
                            pe.wait_ge(c_bank_free, count(it, 4, c_n))
                            for g in range(PAIRS):
                                for b in range(2):
                                    at = slice(64 * b, 64 * (b + 1))
                                    ins = nc.tensor.matmul(pl_c[:, g, at], kv_diag[:, j, b, :], probs_t[:, j, g, at],
                                                           start=True, stop=True)
                            ins.then_inc(contexts_ready[j], 1)
                            c_n += 1
                        elif stage == "project":
                            pe.wait_ge(c_bank_free, count(it, 4, c_n))
                            for g in range(PAIRS):
                                ins = nc.tensor.matmul(pl_c[:, 0:2, :], lat_c_t[:, j, g, :], latent_o_w[:, g, :],
                                                       start=(g == 0), stop=(g == PAIRS - 1))
                            ins.then_inc(l2_proj_ready[j], 1)
                            c_n += 1

        with nc.Block() as block:
            @block.scalar
            def _(act):
                row_roots(act, 2)
                with act.Fori(0, ITERS) as it:
                    for _, j, stage in order_c:
                        if stage == "turn":
                            act.wait_ge(l3_turned[j], count(it, 1, 1))
                            nc.scalar.activation(x2_t[:, j, :, :], pd_turn[j], ACT.Copy).then_inc(x2_t_ready[j], 1)
                row_roots(act, 3)

            @block.vector
            def _(dve):
                row_norms(dve, 2)
                with dve.Fori(0, ITERS) as it:
                    for _, j, stage in order_c:
                        tile = it * SLOTS + j
                        if stage == "norm_in":
                            nc.vector.tensor_scalar(x2[:, j, :], rows[:, bass.ds(tile * HID, HID)], tile_mean(tile),
                                                    tile_rstd[:, bass.ds(tile, 1)], ALU.subtract, ALU.mult).then_inc(x2_ready[j], 1)
                        elif stage == "norm_out":
                            dve.wait_ge(dense_ready[j], count(it, 1, 1))
                            dve.wait_ge(row_stored[j], count(it, 2, 4 * ITERS))
                            nc.vector.tensor_tensor(y_row[:, j, :], pd_dense[j], x2[:, j, :], ALU.add).then_inc(dense_read[j], 1)
                            dve.wait_ge(dense_read[j], count(it, 1, 1))
                            nc.vector.bn_stats(stats[:, j, :], y_row[:, j, :]).then_inc(row_summed[j], 1)
                for j in range(SLOTS):
                    dve.wait_ge(row_stored[j], 6 * ITERS)
                row_norms(dve, 3)
                with dve.Fori(0, ITERS) as it:
                    for j in range(SLOTS):
                        tile = it * SLOTS + j
                        dve.wait_ge(stored[j], count(it, 16, 0))
                        nc.vector.tensor_scalar(out_row[:, j, :], rows[:, bass.ds(tile * HID, HID)], tile_mean(tile),
                                                tile_rstd[:, bass.ds(tile, 1)], ALU.subtract, ALU.mult).then_inc(out_ready[j], 1)

            @block.gpsimd
            def _(pool):
                with pool.Fori(0, ITERS) as it:
                    for _, j, stage in order_c:
                        if stage == "norm_out":
                            store_row(pool, it + 2 * ITERS, j, it)

            @block.tensor
            def _(pe):
                with pe.Fori(0, ITERS) as it:
                    for _, j, stage in order_c:
                        if stage == "turn":
                            pe.wait_ge(x2_ready[j], count(it, 1, 1))
                            pe.wait_ge(x2_t_ready[j], count(it, 1, 0))
                            for t in range(CT):
                                ins = nc.tensor.transpose(pd_turn[j][:, t, :], x2[:, j, P * t:P * (t + 1)], ident[:, :])
                            ins.then_inc(l3_turned[j], 1)
                        elif stage == "dense":
                            pe.wait_ge(x2_t_ready[j], count(it, 1, 1))
                            pe.wait_ge(dense_read[j], count(it, 1, 0))
                            for t in range(CT):
                                nc.tensor.matmul(pd_dense[j], x2_t[:, j, t, :], ffn_wt[:, t, :], start=(t == 0), stop=False)
                            nc.tensor.matmul(pd_dense[j], ones_row[:, :], bias_row[:, :], start=False,
                                             stop=True).then_inc(dense_ready[j], 1)

            @block.sync
            def _(sp):
                with sp.Fori(0, ITERS) as it:
                    for j in range(SLOTS):
                        sp.wait_ge(out_ready[j], count(it, 1, 1))
                        sp.dma_start(out[bass.ds((it * SLOTS + j) * P, P), :], out_row[:, j, :]).then_inc(stored[j], 16)
                for j in range(SLOTS):
                    sp.wait_ge(stored[j], 16 * ITERS)


_INS = ["x", "ctx_512", "L0_attn_memory", "L0_attn_Wq", "L0_attn_Wk", "L0_attn_Wv", "L0_attn_Wo", "L0_attn_log_beta",
        "L0_attn_g_state", "L0_attn_b_state", "L0_attn_g_mem", "L0_attn_b_mem", "L0_xattn_Wq", "L0_xattn_w_kc_q",
        "L0_xattn_w_kc_kv", "L0_xattn_W_qr", "L0_xattn_W_kr", "L0_xattn_Wo", "L0_ffn_weight", "L0_ffn_scale_weight",
        "L0_ffn_bias"]


def rope_tables():
    import numpy as np
    inv_freq = (1.0 / np.float32(10000.0) ** (np.arange(0, XD, 2, dtype=np.float32) / np.float32(XD))).astype(np.float32)
    freqs = np.arange(SEQ, dtype=np.float32)[:, None] * inv_freq[None, :]
    cos = np.repeat(np.cos(freqs), 2, axis=-1)
    sin = np.repeat(np.sin(freqs), 2, axis=-1)
    sin[:, :XD // 2] *= -1.0
    return [np.ascontiguousarray(np.tile(t.astype(np.float32), (2, 2))) for t in (cos, sin)]


def kernel(**inputs):
    import numpy as np
    import concourse.bacc as bacc
    from concourse.bass_utils import run_bass_kernel_spmd

    nc = bacc.Bacc("TRN2", target_bir_lowering=False, num_devices=1)
    arrays, args = {}, []

    def add(name, a):
        arrays[f"in_{name}_dram"] = a
        args.append(nc.dram_tensor(f"in_{name}_dram", a.shape, mybir.dt.from_np(a.dtype), kind="ExternalInput").ap())

    for name in _INS:
        a = np.ascontiguousarray(inputs[name])
        add(name, a.reshape(ROWS, HID) if name == "x" else a)
    cos, sin = rope_tables()
    add("rope_cos", cos)
    add("rope_sin", sin)
    out = nc.dram_tensor("out_0_dram", (ROWS, HID), F32, kind="ExternalOutput").ap()
    decoder_kernel(nc, *args, out)
    r = run_bass_kernel_spmd(nc, [arrays], core_ids=[0])
    return r.results[0]["out_0_dram"].reshape(BATCH, SEQ, HID)
```

```python
from contextlib import ExitStack

import concourse.bass as bass
from concourse import mybir

P = 128
F32 = mybir.dt.float32
I32 = mybir.dt.int32
ALU = mybir.AluOpType
ACT = mybir.ActivationFunctionType
AX_X = mybir.AxisListType.X
RED_MAX = bass.bass_isa.ReduceOp.max
EPS = 1e-5

BATCH, SEQ, HID = 32, 64, 256
ROWS = BATCH * SEQ
TILES = ROWS // P
SLOTS = 4
PASSES = TILES // SLOTS
CT = HID // P
HEADS, MEM = 8, 256
NT = MEM // P
STEPS = 3
XH, XD, XQ, XR = 16, 64, 192, 64
PAIRS = XH // 2
QS = XQ // 2
N_SMALL = 7

U_MAX = 1.0 - MEM ** -0.5
QUICK = dict(evals=4, first=(0.909, 1.202, 0.152), slots=SLOTS)
GENERAL = dict(evals=8, first=(1.0, 1.0, 0.0), slots=1)
LAST_STEP = 3e-3


class Pipeline:

    def __init__(self, stages, period, slots=SLOTS):
        self.slots, self.passes = slots, TILES // slots
        self.order = []
        for j in range(slots):
            for pos, *what in stages:
                at = pos + j * period / slots
                late = at >= period
                self.order.append((at - period if late else at, not late, j, late, tuple(what)))
        self.order.sort(key=lambda r: r[:3])
        self.order = [(j, late, what) for _, _, j, late, what in self.order]

    def play(self, eng, run):
        def last_use(now, k, names):
            uses = [u for u, (_, _, what) in enumerate(self.order) if what[0] in names]
            first, last = isinstance(now, int) and now == 0, isinstance(now, int) and now == self.passes
            here = [u for u in uses if u < k and not (first and self.order[u][1]) and not (last and not self.order[u][1])]
            if here:
                j, late, what = self.order[here[-1]]
                return (now - 1 if late else now), j, what
            if first:
                return None
            j, late, what = self.order[uses[-1]]
            assert not late
            return now - 1, j, what

        def stage(now, k):
            j, late, what = self.order[k]
            run(now - 1 if late else now, lambda *names: last_use(now, k, names), j, what)

        for k, (_, late, _) in enumerate(self.order):
            if not late:
                stage(0, k)
        with eng.Fori(1, self.passes) as now:
            for k in range(len(self.order)):
                stage(now, k)
        for k, (_, late, _) in enumerate(self.order):
            if late:
                stage(self.passes, k)


def memory_pipeline(evals, slots):
    step_len = 4 * evals + 5
    one = [(0.15, "norm_in", 0, 0), (2.0, "turn_in", 0, 0)]
    for s in range(STEPS):
        first = 8 + s * step_len
        last = first + 4 * (evals - 1)
        one += [(first - 1.4, "scores", s, 0), (first - 1.3, "row_max", s, 0)]
        for e in range(evals):
            b = first + 4 * e
            one += [(b, "resid_lo", s, e), (b + 0.1, "resid_hi", s, e), (b + 0.8, "moments", s, e),
                    (b + 0.9, "sums", s, e), (b + 1.65, "root", s, e), (b + 1.95, "inverse", s, e),
                    (b + 2.0, "newton", s, e), (b + 2.75, "clip", s, e)]
        one += [(last + 3.35, "weights", s, 0), (last + 3.7, "turn_weights", s, 0), (last + 4.25, "square_weights", s, 0)]
    one += [(last + 4.55, "project", 0, 0), (last + 7.45, "norm_out", 0, 0)]
    return Pipeline(one, STEPS * step_len, slots)


def latent_pipeline():
    names = ["fetch", "turn_x", "queries", "scores", "shift", "exp", "sum", "normalise", "turn_probs", "contexts",
             "project", "residual"]
    return Pipeline([(k, n) for k, n in enumerate(names)], len(names))


def dense_pipeline():
    return Pipeline([(0, "norm_in"), (1, "turn"), (2.6, "dense"), (3.3, "residual")], 4)


def prep_jobs():
    jobs = [("wk_t", i) for i in range(2)] + [("wv_t", i) for i in range(2)] + [("mem_t", 0)]
    jobs += [("k_t", i) for i in range(4)] + [("v_t", i) for i in range(4)]
    jobs += [("wo_t", i) for i in range(4)]
    jobs += [("wqr_t", i) for i in range(6)] + [("wkr_t", i) for i in range(2)]
    jobs += [("g", i) for i in range(4)]
    jobs += [("xwo_t", i) for i in range(8)]
    for i in range(4):
        jobs += [("j", 4 * i + k) for k in range(4)] + [("a", i)]
    jobs += [("b", i) for i in range(4)] + [("ffn_t", 0)]
    jobs += [("score_in", h) for h in range(HEADS)]
    jobs += [("score_step", h) for h in range(HEADS)]
    jobs += [("value_out", h) for h in range(HEADS)]
    return jobs


def decoder_kernel(nc, x, ctx_kv, memory, Wq, Wk, Wv, Wo, log_beta, g_state, b_state, g_mem, b_mem,
                   xWq, w_kc_q, w_kc_kv, W_qr, W_kr, xWo, ffn_w, ffn_scale, ffn_bias,
                   rope_cos, rope_sin, out):
    jobs = prep_jobs()
    job_no = {job: n for n, job in enumerate(jobs)}

    with ExitStack() as ctx:
        def sb(name, shape, dt=F32):
            return ctx.enter_context(nc.sbuf_tensor(name, shape, dt))

        def sem(name):
            return ctx.enter_context(nc.semaphore(name))

        def per_slot(name):
            return [sem(f"{name}{j}") for j in range(SLOTS)]

        rows = sb("rows", [P, TILES * HID])
        weights_s = sb("weights_s", [P, 3 * HEADS * 2 * HID])
        latent_q_w = sb("latent_q_w", [P, CT, XH * XD])
        latent_o_w = sb("latent_o_w", [P, PAIRS, HID])
        ffn_wt = sb("ffn_wt", [P, CT, HID])
        ident = sb("ident", [P, P])
        bias_rows = sb("bias_rows", [P, HID])
        beta = sb("beta", [P, HEADS])
        g_col, b_col = sb("g_col", [P, CT]), sb("b_col", [P, CT])
        gm_col, bm_col = sb("gm_col", [P, 1]), sb("bm_col", [P, 1])
        ffn_s = sb("ffn_s", [P, CT])
        cos_sb, sin_sb = sb("cos_sb", [P, 2, XD]), sb("sin_sb", [P, 2, XD])
        stats = sb("stats", [P, SLOTS, 6])
        mem_stats, mem_mv = sb("mem_stats", [P, NT, 6]), sb("mem_mv", [P, NT, 2])
        mem_var, mem_std, mem_rstd = (sb(n, [P, NT]) for n in ("mem_var", "mem_std", "mem_rstd"))
        tile_stats = sb("tile_stats", [P, TILES, 6])
        tile_mv = sb("tile_mv", [P, TILES, 2])
        tile_var, tile_std, tile_rstd = (sb(n, [P, TILES]) for n in ("tile_var", "tile_std", "tile_rstd"))
        small = {n: sb(n, [P, SLOTS, HEADS]) for n in
                 ("neg_max", "one_less_max", "resid_sum", "sum_mean", "sq_sum", "sq_root", "inv_sum", "gap", "delta",
                  "first_delta", "neg_u", "neg_u_raw")}
        moments = sb("moments", [P, SLOTS, HEADS, 3])
        step2, step4, unsettled = (sb(n, [P, SLOTS, HEADS]) for n in ("step2", "step4", "unsettled"))
        worst, worst_all = sb("worst", [P, 1]), sb("worst_all", [P, 1])
        too_far = sb("too_far", [P, 1])
        flag = sb("flag", [P, 1], I32)
        neg_u_start, first_scale = sb("neg_u_start", [P, 2, HEADS]), sb("first_scale", [P, 2, HEADS])
        tile_mv_flat = tile_mv[:, :, :].rearrange("p t k -> p (t k)")
        tile_stats_flat = tile_stats[:, :, :].rearrange("p t k -> p (t k)")

        work = sb("work", [P, 27648])

        def carve(region, at, *dims):
            n = 1
            for d in dims:
                n *= d
            view = region[:, at:at + n]
            if len(dims) == 1:
                return view
            names = "abcd"[:len(dims)]
            return view.rearrange(f"p ({' '.join(names)}) -> p {' '.join(names)}",
                                  **{k: d for k, d in zip(names[1:], dims[1:])})

        score_in_w = carve(weights_s, 0, HEADS, CT, MEM)
        score_step_w = carve(weights_s, 4096, HEADS, NT, MEM)
        value_out_w = carve(weights_s, 8192, HEADS, NT, HID)
        xwo_raw = carve(weights_s, 0, CT, XH * P)
        xwq_raw = carve(weights_s, 4096, XH, HID)
        kcq_raw = carve(weights_s, 8192, XH, XQ)
        ffn_raw = carve(weights_s, 11264, CT, HID)
        ffn_scaled = carve(weights_s, 11776, CT, HID)
        kckv_pad = carve(rows, 0, XH, P)
        wqr_raw = carve(rows, 2048, 24, XR)
        wkr_raw = carve(rows, 3584, 8, XR)

        mem_raw = carve(work, 0, NT, P)
        mem_hat = carve(work, 256, NT, P)
        mem_t = carve(work, 512, MEM)
        wk_raw = carve(work, 1024, HEADS, P)
        wv_raw = carve(work, 2048, HEADS, P)
        wq_raw = carve(work, 3072, HEADS, HID)
        wo_raw = carve(work, 5120, CT, HEADS * P)
        wk_t = carve(work, 7168, HEADS * P)
        wv_t = carve(work, 8192, HEADS * P)
        k_t = carve(work, 9216, HEADS, MEM)
        v_t = carve(work, 11264, HEADS, MEM)
        wo_t = carve(work, 13312, HEADS, HID)
        xwo_t = carve(work, 15360, XH, HID)
        wqr_t = carve(work, 19456, XH * XQ)
        wkr_t = carve(work, 22528, XH * XD)
        g_sb = carve(work, 23552, XH, 2, XD)
        j_sb = carve(work, 25600, 4, 2 * HID)

        resid0 = carve(work, 0, SLOTS, HEADS, MEM)
        resid = carve(work, 8192, SLOTS, HEADS, MEM)
        weights_t = carve(work, 16384, SLOTS, HEADS, NT * P)
        x_hat = carve(work, 24576, SLOTS, HID)
        x_hat_t = carve(work, 25600, SLOTS, CT, P)
        y_row = carve(work, 26624, SLOTS, HID)
        lat_q_t = carve(work, 0, SLOTS, PAIRS, P)
        probs = carve(work, 4096, SLOTS, XH, XD)
        probs_t = carve(work, 8192, SLOTS, PAIRS, P)
        lat_c_t = carve(work, 12288, SLOTS, PAIRS, P)
        lat_x = carve(work, 16384, SLOTS, HID)
        lat_x_t = carve(work, 17408, SLOTS, CT, P)
        kv_in = carve(work, 18432, SLOTS, 2, XD)
        kv_cos = carve(work, 18944, SLOTS, 2, XD)
        kv_rot = carve(work, 19456, SLOTS, 2, XD)
        kv_diag = carve(work, 19968, SLOTS, 2, P)
        kv_diag_t = carve(work, 20992, SLOTS, 2, P)
        row_nmax, row_sum, row_inv = (carve(work, 22016 + 64 * k, SLOTS, XH) for k in range(3))
        x2 = carve(work, 0, SLOTS, HID)
        x2_t = carve(work, 1024, SLOTS, CT, P)
        out_row = carve(work, 2048, SLOTS, HID)
        x2_bias = carve(work, 3072, SLOTS, HID)

        banks = ctx.enter_context(nc.psum_tensor("banks", [P, 8, 512], F32))

        def pbank(b, n, *dims):
            view = banks[:, b:b + n, :].rearrange("p b n -> p (b n)")
            if not dims:
                return view
            names = "abc"[:len(dims)]
            return view.rearrange(f"p ({' '.join(names)}) -> p {' '.join(names)}",
                                  **{k: d for k, d in zip(names[1:], dims[1:])})

        ps_scores = pbank(0, 4, HEADS, MEM)
        ps_turn = pbank(4, 4, HEADS, NT, P)
        ps_turn_flat = pbank(4, 4)
        pl_q, pl_s, pl_p, pl_c = pbank(0, 2, PAIRS, P), pbank(2, 2, XH, XD), pbank(4, 2, PAIRS, P), pbank(6, 2, PAIRS, P)
        pd_turn = [pbank(j, 1, 4, P)[:, 0:CT, :] for j in range(SLOTS)]
        pd_dense = [pbank(4 + j, 1)[:, 0:HID] for j in range(SLOTS)]

        ld_mem, ld_affine, ld_kv, ld_wo, ld_wq, ld_small, ld_qr, ld_xo, ld_xq, ld_x, ld_ffn, ld_pad = (sem(n) for n in
            ("ld_mem", "ld_affine", "ld_kv", "ld_wo", "ld_wq", "ld_small", "ld_qr", "ld_xo", "ld_xq", "ld_x", "ld_ffn", "ld_pad"))
        setup = sem("setup")
        prep_filled = sem("prep_filled")
        prep_emptied = [sem("prep_emptied_act"), sem("prep_emptied_dve")]
        prep_chain = sem("prep_chain")
        mem_var_ready, mem_std_ready, mem_ready, beta_ready, pad_ready, ffn_scaled_ready = (sem(n) for n in
            ("mem_var_ready", "mem_std_ready", "mem_ready", "beta_ready", "pad_ready", "ffn_scaled_ready"))
        x_stats_ready = sem("x_stats_ready")
        row_summed, row_stored = per_slot("row_summed"), per_slot("row_stored")
        norm_step, tile_var_ready, tile_std_ready = sem("norm_step"), sem("tile_var_ready"), sem("tile_std_ready")
        flag_step = sem("flag_step")
        kv_read = per_slot("kv_read")

        layer_1_sems = []

        def slot_sems(scope, name, slots=SLOTS):
            return [scope.enter_context(nc.semaphore(f"{name}{j}")) for j in range(slots)]

        def load_x(sp, done):
            sp.dma_start(rows[:, :].rearrange("p (t c) -> p t c", c=HID),
                         x.rearrange("(t p) c -> p t c", p=P)).then_inc(done, 16)

        def x_stats(dve, loaded, tiles=range(TILES)):
            dve.wait_ge(loaded, 16)
            for t in tiles:
                ins = nc.vector.bn_stats(tile_stats[:, t, :], rows[:, HID * t:HID * (t + 1)])
            ins.then_inc(x_stats_ready, 1)

        def row_norms(dve, n, step, var_ready, std_ready):
            for t in range(TILES):
                ins = nc.vector.bn_aggr(tile_mv[:, t, :], tile_stats[:, t, :])
            ins.then_inc(step, 1)
            dve.wait_ge(step, 2 * n + 1)
            nc.vector.tensor_scalar(tile_var[:, :], tile_mv[:, :, 1], EPS, None, ALU.add).then_inc(var_ready, 1)
            dve.wait_ge(std_ready, n + 1)
            nc.vector.reciprocal(tile_rstd[:, :], tile_std[:, :]).then_inc(step, 1)
            dve.wait_ge(step, 2 * n + 2)

        def row_roots(act, n, var_ready, std_ready):
            act.wait_ge(var_ready, n + 1)
            nc.scalar.activation(tile_std[:, :], tile_var[:, :], ACT.Sqrt).then_inc(std_ready, 1)

        def at_tile(tile):
            if isinstance(tile, int):
                return (rows[:, tile * HID:(tile + 1) * HID], tile_mv[:, tile, 0:1], tile_rstd[:, tile:tile + 1])
            return (rows[:, bass.ds(tile * HID, HID)], tile_mv_flat[:, bass.ds(tile * 2, 1)],
                    tile_rstd[:, bass.ds(tile, 1)])

        def store_stats(pool, summed, stored_, tile, total, j):
            pool.wait_ge(summed[j], total + 1)
            if isinstance(tile, int):
                st = tile_stats[:, tile, :]
            else:
                st = tile_stats_flat[:, bass.ds(tile * 6, 6)]
            nc.gpsimd.tensor_copy(st, stats[:, j, :]).then_inc(stored_[j], 1)

        def store_row(pool, summed, stored_, tile, total, j):
            store_stats(pool, summed, stored_, tile, total, j)
            nc.gpsimd.tensor_copy(at_tile(tile)[0], y_row[:, j, :]).then_inc(stored_[j], 1)

        with nc.Block() as block:
            @block.sync
            def _(sp):
                sp.dma_start(mem_raw, memory.rearrange("(t p) c -> p t c", p=P)).then_inc(ld_mem, 16)
                for col, src in ((gm_col, g_mem), (bm_col, b_mem)):
                    sp.dma_start(col[:, :], src.rearrange("(t p) -> p t", p=P),
                                 allow_slow_non_contiguous=True).then_inc(ld_affine, 16)
                sp.dma_start(wk_raw, Wk.rearrange("(h p) c -> p h c", p=P)).then_inc(ld_kv, 16)
                sp.dma_start(wv_raw, Wv.rearrange("(h p) c -> p h c", p=P)).then_inc(ld_kv, 16)
                sp.dma_start(wo_raw, Wo.rearrange("(t p) c -> p t c", p=P)).then_inc(ld_wo, 16)
                sp.dma_start(wqr_raw, W_qr.rearrange("h q r -> (h q) r").rearrange("(t p) r -> p t r", p=P)).then_inc(ld_qr, 16)
                sp.dma_start(wkr_raw, W_kr.rearrange("h d r -> (h d) r").rearrange("(t p) r -> p t r", p=P)).then_inc(ld_qr, 16)
                sp.dma_start(xwo_raw, xWo.rearrange("(t p) c -> p t c", p=P)).then_inc(ld_xo, 16)
                sp.dma_start(xwq_raw, xWq.rearrange("(h p) c -> p h c", p=P)).then_inc(ld_xq, 16)
                sp.dma_start(kcq_raw, w_kc_q.rearrange("h k q -> k h q")).then_inc(ld_xq, 16)
                sp.dma_start(ffn_raw, ffn_w.rearrange("(t p) c -> p t c", p=P)).then_inc(ld_ffn, 16)
                sp.dma_start(wq_raw, Wq.rearrange("(h p) c -> p h c", p=P)).then_inc(ld_wq, 16)
                sp.wait_ge(pad_ready, 1)
                kp = kckv_pad.rearrange("p (g two) d -> p g two d", two=2)
                src = w_kc_kv.rearrange("(g two) k d -> k g two d", two=2)
                for odd in range(2):
                    sp.dma_start(kp[:, :, odd, odd * XD:(odd + 1) * XD], src[:, :, odd, :]).then_inc(ld_pad, 16)
                n_made = job_no[("b", 3)] + 1
                sp.wait_ge(prep_emptied[0], (n_made + 1) // 2)
                sp.wait_ge(prep_emptied[1], n_made // 2)
                load_x(sp, ld_x)

            @block.gpsimd
            def _(pool):
                nc.gpsimd.memset(kckv_pad, 0.0).then_inc(pad_ready, 1)
                pool.dma_start(beta[:, :], log_beta.rearrange("(a h) -> a h", a=1).to_broadcast([P, HEADS])).then_inc(ld_small, 16)
                for col, src in ((g_col, g_state), (b_col, b_state), (ffn_s, ffn_scale)):
                    pool.dma_start(col[:, :], src.rearrange("(t p) -> p t", p=P),
                                   allow_slow_non_contiguous=True).then_inc(ld_small, 16)
                pool.dma_start(bias_rows[:, :], ffn_bias.rearrange("(a n) -> a n", a=1).to_broadcast([P, HID])).then_inc(ld_small, 16)
                pool.dma_start(cos_sb[:, :, :], rope_cos.rearrange("p (b d) -> p b d", b=2)).then_inc(ld_small, 16)
                pool.dma_start(sin_sb[:, :, :], rope_sin.rearrange("p (b d) -> p b d", b=2)).then_inc(ld_small, 16)
                nc.gpsimd.memset(ident[:, :], 0.0).then_inc(setup, 1)
                pool.wait_ge(setup, 1)
                nc.gpsimd.affine_select(out=ident[:, :], in_=ident[:, :], compare_op=ALU.not_equal, fill=1.0, base=0,
                                        pattern=[[-1, P]], channel_multiplier=1).then_inc(setup, 1)
                nc.gpsimd.memset(unsettled[:, :, :], 0.0).then_inc(setup, 1)
                for n, path in enumerate((QUICK, GENERAL)):
                    nc.gpsimd.memset(neg_u_start[:, n, :], -path["first"][2]).then_inc(setup, 1)
                    nc.gpsimd.memset(first_scale[:, n, :], path["first"][0]).then_inc(setup, 1)
                for sems, n in ((row_stored, 2), (kv_read, 1)):
                    for s in sems:
                        pool.sem_inc(s, n)
                pool.wait_ge(ld_small, 16 * N_SMALL)
                pool.wait_ge(setup, 7)

            def evacuate(eng, which):
                def copy(dst, src):
                    if which == 0:
                        return nc.scalar.activation(dst, src, ACT.Copy)
                    return nc.vector.tensor_copy(dst, src)

                def scaled(dst, src, col):
                    if which == 0:
                        return nc.scalar.activation(dst, src, ACT.Copy, scale=col)
                    return nc.vector.tensor_scalar(dst, src, col, None, ALU.mult)

                for n, (kind, i) in enumerate(jobs):
                    if n % 2 != which:
                        continue
                    eng.wait_ge(prep_filled, n + 1)
                    bank = banks[:, n % 8, :]
                    half = bank.rearrange("p (a b) -> p a b", a=2)
                    if kind == "mem_t":
                        eng.wait_ge(ld_affine, 32)
                        ins = nc.scalar.activation(mem_t, bank[:, 0:MEM], ACT.Identity,
                                                   scale=gm_col[:, 0:1], bias=bm_col[:, 0:1])
                    elif kind == "wk_t":
                        ins = copy(wk_t[:, 512 * i:512 * (i + 1)], bank)
                    elif kind == "wv_t":
                        ins = copy(wv_t[:, 512 * i:512 * (i + 1)], bank)
                    elif kind == "k_t":
                        ins = copy(k_t[:, 2 * i:2 * i + 2, :], half)
                    elif kind == "v_t":
                        ins = copy(v_t[:, 2 * i:2 * i + 2, :], half)
                    elif kind == "wo_t":
                        ins = copy(wo_t[:, 2 * i:2 * i + 2, :], half)
                    elif kind == "score_in":
                        if which == 0 and i in (0, 1):
                            eng.wait_ge(ld_small, 16 * N_SMALL)
                            nc.scalar.activation(beta[:, :], beta[:, :], ACT.Exp).then_inc(beta_ready, 1)
                            eng.wait_ge(beta_ready, 1)
                            nc.scalar.activation(beta[:, :], beta[:, :], ACT.Copy, scale=0.5).then_inc(beta_ready, 1)
                        if i in (0, 1):
                            eng.wait_ge(beta_ready, 2)
                        ins = scaled(score_in_w[:, i, :, :], half, beta[:, i:i + 1])
                    elif kind == "score_step":
                        ins = scaled(score_step_w[:, i, :, :], half, beta[:, i:i + 1])
                    elif kind == "value_out":
                        ins = copy(value_out_w[:, i, :, :], half)
                    elif kind == "wqr_t":
                        ins = copy(wqr_t[0:XR, 512 * i:512 * (i + 1)], bank[0:XR, :])
                    elif kind == "wkr_t":
                        ins = copy(wkr_t[0:XR, 512 * i:512 * (i + 1)], bank[0:XR, :])
                    elif kind == "g":
                        ins = copy(g_sb[0:QS, 4 * i:4 * i + 4, :, :],
                                   bank[0:QS, :].rearrange("p (h t d) -> p h t d", h=4, t=2))
                    elif kind == "xwo_t":
                        if which == 1 and i in (0, 1):
                            eng.wait_ge(ld_ffn, 16)
                            eng.wait_ge(ld_small, 16 * N_SMALL)
                            for t in range(CT):
                                nc.vector.tensor_scalar(ffn_scaled[:, t, :], ffn_raw[:, t, :], ffn_s[:, t:t + 1], None,
                                                        ALU.mult).then_inc(ffn_scaled_ready, 1)
                        ins = copy(xwo_t[:, 2 * i:2 * i + 2, :], half)
                    elif kind == "j":
                        ins = copy(j_sb[0:QS, i % 4, :], bank[0:QS, :])
                    elif kind == "a":
                        ins = copy(latent_q_w[:, :, 4 * XD * i:4 * XD * (i + 1)], half)
                    elif kind == "b":
                        ins = copy(latent_o_w[:, 2 * i:2 * i + 2, :], half)
                    elif kind == "ffn_t":
                        ins = copy(ffn_wt[:, :, :], half)
                    ins.then_inc(prep_emptied[which], 1)
                    if which == 1 and kind == "value_out":
                        x_stats(eng, ld_x, range(i // 2 * 4, i // 2 * 4 + 4))

            @block.scalar
            def _(act):
                act.wait_ge(mem_var_ready, 1)
                nc.scalar.activation(mem_std[:, :], mem_var[:, :], ACT.Sqrt).then_inc(mem_std_ready, 1)
                evacuate(act, 0)

            @block.vector
            def _(dve):
                dve.wait_ge(ld_mem, 16)
                for t in range(NT):
                    nc.vector.bn_stats(mem_stats[:, t, :], mem_raw[:, t, :]).then_inc(prep_chain, 1)
                dve.wait_ge(prep_chain, NT)
                for t in range(NT):
                    nc.vector.bn_aggr(mem_mv[:, t, :], mem_stats[:, t, :]).then_inc(prep_chain, 1)
                dve.wait_ge(prep_chain, 2 * NT)
                nc.vector.tensor_scalar(mem_var[:, :], mem_mv[:, :, 1], EPS, None, ALU.add).then_inc(mem_var_ready, 1)
                dve.wait_ge(mem_std_ready, 1)
                nc.vector.reciprocal(mem_rstd[:, :], mem_std[:, :]).then_inc(prep_chain, 1)
                dve.wait_ge(prep_chain, 2 * NT + 1)
                for t in range(NT):
                    nc.vector.tensor_scalar(mem_hat[:, t, :], mem_raw[:, t, :], mem_mv[:, t, 0:1], mem_rstd[:, t:t + 1],
                                            ALU.subtract, ALU.mult).then_inc(mem_ready, 1)
                evacuate(dve, 1)

            @block.tensor
            def _(pe):
                def emptied(kind, i):
                    n = job_no[(kind, i)] + 1
                    pe.wait_ge(prep_emptied[0], (n + 1) // 2)
                    if n // 2:
                        pe.wait_ge(prep_emptied[1], n // 2)

                pe.wait_ge(setup, 2)
                for n, (kind, i) in enumerate(jobs):
                    if n >= 8:
                        pe.wait_ge(prep_emptied[n % 2], (n - 8) // 2 + 1)
                    bank = banks[:, n % 8, :]
                    mm = []
                    T = nc.tensor.transpose

                    def M(out, lhsT, rhs, start, stop):
                        return nc.tensor.matmul(out, lhsT, rhs, start=start, stop=stop)

                    if kind == "mem_t":
                        pe.wait_ge(mem_ready, NT)
                        for t in range(NT):
                            ins = T(bank[:, P * t:P * (t + 1)], mem_hat[:, t, :], ident[:, :])
                    elif kind in ("wk_t", "wv_t"):
                        pe.wait_ge(ld_kv, 32)
                        raw = wk_raw if kind == "wk_t" else wv_raw
                        for q in range(4):
                            ins = T(bank[:, P * q:P * (q + 1)], raw[:, 4 * i + q, :], ident[:, :])
                    elif kind in ("k_t", "v_t"):
                        emptied("mem_t", 0)
                        w = wk_t if kind == "k_t" else wv_t
                        for q in range(2):
                            h = 2 * i + q
                            ins = M(bank[:, 256 * q:256 * (q + 1)], w[:, P * h:P * (h + 1)], mem_t, True, True)
                    elif kind == "wo_t":
                        pe.wait_ge(ld_wo, 16)
                        for q in range(2):
                            h = 2 * i + q
                            for t in range(CT):
                                ins = T(bank[:, 256 * q + P * t:256 * q + P * (t + 1)],
                                        wo_raw[:, t, P * h:P * (h + 1)], ident[:, :])
                    elif kind == "score_in":
                        pe.wait_ge(ld_wq, 16)
                        for t in range(CT):
                            ins = M(bank[:, 256 * t:256 * (t + 1)], wq_raw[:, i, P * t:P * (t + 1)], k_t[:, i, :], True, True)
                    elif kind == "score_step":
                        for t in range(NT):
                            ins = M(bank[:, 256 * t:256 * (t + 1)], v_t[:, i, P * t:P * (t + 1)], k_t[:, i, :], True, True)
                    elif kind == "value_out":
                        for t in range(NT):
                            ins = M(bank[:, 256 * t:256 * (t + 1)], v_t[:, i, P * t:P * (t + 1)], wo_t[:, i, :], True, True)
                    elif kind == "wqr_t":
                        pe.wait_ge(ld_qr, 32)
                        for q in range(4):
                            ins = T(bank[0:XR, P * q:P * (q + 1)], wqr_raw[:, 4 * i + q, :], ident[:, :])
                    elif kind == "wkr_t":
                        for q in range(4):
                            ins = T(bank[0:XR, P * q:P * (q + 1)], wkr_raw[:, 4 * i + q, :], ident[:, :])
                    elif kind == "g":
                        emptied("wkr_t", 1)
                        for q in range(4):
                            h = 4 * i + q
                            for t in range(2):
                                ins = M(bank[0:QS, P * q + XD * t:P * q + XD * (t + 1)],
                                        wqr_t[0:XR, XQ * h + QS * t:XQ * h + QS * (t + 1)],
                                        wkr_t[0:XR, XD * h:XD * (h + 1)], True, True)
                    elif kind == "xwo_t":
                        pe.wait_ge(ld_xo, 16)
                        for q in range(2):
                            h = 2 * i + q
                            for t in range(CT):
                                ins = T(bank[:, 256 * q + P * t:256 * q + P * (t + 1)],
                                        xwo_raw[:, t, P * h:P * (h + 1)], ident[:, :])
                    elif kind == "j":
                        if i >= 4:
                            emptied("a", i // 4 - 1)
                        pe.wait_ge(ld_xq, 32)
                        for t in range(2):
                            ins = M(bank[0:QS, 256 * t:256 * (t + 1)], kcq_raw[:, i, QS * t:QS * (t + 1)],
                                    xwq_raw[:, i, :], True, True)
                    elif kind == "a":
                        emptied("j", 4 * i + 3)
                        for c in range(CT):
                            for q in range(4):
                                h = 4 * i + q
                                for t in range(2):
                                    ins = M(bank[:, 256 * c + XD * q:256 * c + XD * (q + 1)],
                                            j_sb[0:QS, h % 4, 256 * t + P * c:256 * t + P * (c + 1)],
                                            g_sb[0:QS, h, t, :], t == 0, t == 1)
                    elif kind == "b":
                        pe.wait_ge(ld_pad, 32)
                        emptied("xwo_t", 7)
                        for q in range(2):
                            g = 2 * i + q
                            for odd in range(2):
                                ins = M(bank[:, 256 * q:256 * (q + 1)], kckv_pad[:, 2 * g + odd, :],
                                        xwo_t[:, 2 * g + odd, :], odd == 0, odd == 1)
                    elif kind == "ffn_t":
                        pe.wait_ge(ffn_scaled_ready, CT)
                        for c in range(CT):
                            for t in range(CT):
                                ins = T(bank[:, 256 * c + P * t:256 * c + P * (t + 1)],
                                        ffn_scaled[:, t, P * c:P * (c + 1)], ident[:, :])
                    ins.then_inc(prep_filled, 1)

        def memory_attention(block, tag, evals, first, slots, always):
            pipe = memory_pipeline(evals, slots)

            def layer_sem(name):
                layer_1_sems.append(nc.alloc_semaphore(name=f"{tag}_{name}"))
                return layer_1_sems[-1]

            def layer_sems(name):
                return [layer_sem(f"{name}{j}") for j in range(slots)]

            hat_ready, turned_in, scores_ready, offset_ready = (layer_sems(n) for n in
                ("hat_ready", "turned_in", "scores_ready", "offset_ready"))
            resid_ready, moments_ready, sum_ready, sum_mean_ready, sq_ready, inv_ready, root_ready, u_ready = (
                layer_sems(n) for n in ("resid_ready", "moments_ready", "sum_ready", "sum_mean_ready", "sq_ready",
                                        "inv_ready", "root_ready", "u_ready"))
            weights_ready, weights_turned, proj_ready = (layer_sems(n) for n in
                ("weights_ready", "weights_turned", "proj_ready"))
            scores_used = layer_sems("scores_used")
            in_emptied = layer_sems("in_emptied")
            turn_emptied = layer_sems("turn_emptied")
            max_ready, pool_step, settle_step = layer_sems("max_ready"), layer_sems("pool_step"), layer_sems("settle_step")
            if always:
                summed, stored_, step, var_ready, std_ready = row_summed, row_stored, norm_step, tile_var_ready, tile_std_ready
            else:
                summed, stored_ = layer_sems("row_summed"), layer_sems("row_stored")
                step, var_ready, std_ready = (layer_sem(n) for n in ("norm_step", "var_ready", "std_ready"))
                x_loaded = layer_sem("x_loaded")
            PER = 3
            QUARTERS = 4
            T_PASS = QUARTERS * (STEPS + 1)

            def turn_count(p, stage, s, n):
                use = {"turn_weights": s, "project": STEPS}[stage]
                return p * T_PASS + (use * QUARTERS + n)

            def turn_free(pe, before, q):
                use = before("turn_in", "turn_weights", "project")
                if use:
                    p, j, (stage, s, _) = use
                    if stage == "turn_in":
                        pe.wait_ge(in_emptied[j], p * CT + CT)
                        return
                    pe.wait_ge(turn_emptied[j], turn_count(p, stage, s, q + 1 if stage == "turn_weights" else QUARTERS))

            def pool_count(p, s, e, n):
                return p * (STEPS * (evals * PER + 1)) + (s * (evals * PER + 1) + e * PER + (1 if e else 0) + n)

            def eval_count(p, s, e):
                return p * (STEPS * evals) + (s * evals + e + 1)

            def scores_count(p, s, n):
                return p * (STEPS * HEADS) + (s * HEADS + n)
            fa, fb, _ = first
            tag_no = 0 if always else 1

            def part(engine):
                def wrap(body):
                    def run(eng):
                        if always:
                            return body(eng)
                        asked = eng.alloc_register(f"{tag}_asked")
                        eng.reg_load(asked, flag[0:1, 0:1])
                        with eng.If_ne(asked, 0):
                            body(eng)
                    return engine(run)
                return wrap

            if not always:
                @part(block.sync)
                def _(sp):
                    load_x(sp, x_loaded)

            @part(block.scalar)
            def _(act):
                row_roots(act, 0, var_ready, std_ready)

                def run(p, before, j, what):
                    stage, s, e = what
                    if stage == "turn_in":
                        act.wait_ge(turned_in[j], p + 1)
                        for t in range(CT):
                            nc.scalar.activation(x_hat_t[:, j, t, :], ps_turn_flat[:, P * t:P * (t + 1)], ACT.Identity,
                                                 scale=g_col[:, t:t + 1], bias=b_col[:, t:t + 1]).then_inc(in_emptied[j], 1)
                    elif stage in ("resid_lo", "resid_hi"):
                        half = range(0, 4) if stage == "resid_lo" else range(4, HEADS)
                        if e == 0:
                            act.wait_ge(offset_ready[j], p * STEPS + (s + 1))
                            for h in half:
                                nc.scalar.activation(resid0[:, j, h, :], ps_scores[:, h, :], ACT.Relu,
                                                     bias=small["one_less_max"][:, j, h:h + 1]).then_inc(scores_used[j], 1)
                        else:
                            act.wait_ge(u_ready[j], eval_count(p, s, e - 1))
                            for h in half:
                                nc.scalar.activation(resid[:, j, h, :], resid0[:, j, h, :], ACT.Relu,
                                                     bias=small["neg_u"][:, j, h:h + 1]).then_inc(resid_ready[j], 1)
                    elif stage == "root":
                        act.wait_ge(sq_ready[j], eval_count(p, s, e))
                        nc.scalar.activation(small["sq_root"][:, j, :], small["sq_sum"][:, j, :], ACT.Sqrt,
                                             scale=(fb / fa) ** 2 if e == 0 else 1.0).then_inc(root_ready[j], 1)
                    elif stage == "square_weights":
                        for q in range(4):
                            act.wait_ge(weights_turned[j], p * (STEPS * 4) + (s * 4 + q + 1))
                            nc.scalar.activation(weights_t[:, j, 2 * q:2 * q + 2, :], ps_turn_flat[:, 512 * q:512 * (q + 1)]
                                                 .rearrange("p (h n) -> p h n", h=2), ACT.Square).then_inc(turn_emptied[j], 1)
                pipe.play(act, run)

            @part(block.vector)
            def _(dve):
                if not always:
                    x_stats(dve, x_loaded)
                    dve.wait_ge(x_stats_ready, 5)
                row_norms(dve, 0, step, var_ready, std_ready)

                def run(p, before, j, what):
                    stage, s, e = what
                    if stage == "norm_in":
                        src, mean, rstd = at_tile(p * slots + j)
                        nc.vector.tensor_scalar(x_hat[:, j, :], src, mean, rstd, ALU.subtract, ALU.mult).then_inc(hat_ready[j], 1)
                    elif stage == "row_max":
                        for q in range(4):
                            dve.wait_ge(scores_ready[j], p * (STEPS * 4) + (s * 4 + q + 1))
                            ins = nc.vector.tensor_reduce(small["neg_max"][:, j, 2 * q:2 * q + 2],
                                                          ps_scores[:, 2 * q:2 * q + 2, :], AX_X, ALU.max, negate=True)
                        ins.then_inc(max_ready[j], 1)
                        dve.wait_ge(max_ready[j], p * STEPS + (s + 1))
                        nc.vector.tensor_scalar(small["one_less_max"][:, j, :], small["neg_max"][:, j, :], 1.0, None,
                                                ALU.add).then_inc(offset_ready[j], 1)
                    elif stage == "moments":
                        for h in range(0, HEADS, 2):
                            if e == 0:
                                dve.wait_ge(scores_used[j], scores_count(p, s, h + 2))
                            else:
                                dve.wait_ge(resid_ready[j], p * (STEPS * (evals - 1) * HEADS) +
                                            ((s * (evals - 1) + e - 1) * HEADS + h + 2))
                            r = (resid if e else resid0)[:, j, h:h + 2, :]
                            ins = nc.vector.bn_stats(moments[:, j, h:h + 2, :].rearrange("p h k -> p (h k)"),
                                                     r.rearrange("p h n -> p n h"))
                        ins.then_inc(moments_ready[j], 1)
                    elif stage == "inverse":
                        dve.wait_ge(sum_ready[j], eval_count(p, s, e))
                        nc.vector.reciprocal(small["inv_sum"][:, j, :], small["resid_sum"][:, j, :]).then_inc(inv_ready[j], 1)
                    elif stage == "clip":
                        dve.wait_ge(pool_step[j], pool_count(p, s, e, PER + (e == 0)))
                        nc.vector.tensor_scalar(small["neg_u"][:, j, :], small["neg_u_raw"][:, j, :], 0.0, -U_MAX,
                                                ALU.min, ALU.max).then_inc(u_ready[j], 1)
                    elif stage == "weights":
                        dve.wait_ge(u_ready[j], eval_count(p, s, evals - 1))
                        for h in range(HEADS):
                            ins = nc.vector.tensor_scalar(resid[:, j, h, :], resid0[:, j, h, :],
                                                          small["neg_u"][:, j, h:h + 1], 0.0, ALU.add, ALU.max)
                            if h % 2:
                                ins.then_inc(weights_ready[j], 1)
                    elif stage == "norm_out":
                        src, _, _ = at_tile(p * slots + j)
                        dve.wait_ge(proj_ready[j], p + 1)
                        dve.wait_ge(stored_[j], p * 2 + 2)
                        nc.vector.tensor_tensor(y_row[:, j, :], ps_turn_flat[:, 0:HID], src, ALU.add).then_inc(turn_emptied[j], QUARTERS)
                        dve.wait_ge(turn_emptied[j], turn_count(p, "project", 0, QUARTERS))
                        nc.vector.bn_stats(stats[:, j, :], y_row[:, j, :]).then_inc(summed[j], 1)
                pipe.play(dve, run)

            @part(block.gpsimd)
            def _(pool):
                if not always:
                    for j in range(slots):
                        pool.sem_inc(stored_[j], 2)
                def run(p, before, j, what):
                    stage, s, e = what
                    if stage == "norm_out":
                        store_row(pool, summed, stored_, p * slots + j, p, j)
                    v = {k: t[:, j, :] for k, t in small.items()}
                    if stage == "sums":
                        pool.wait_ge(moments_ready[j], eval_count(p, s, e))
                        nc.gpsimd.tensor_tensor(v["resid_sum"], moments[:, j, :, 0], moments[:, j, :, 1],
                                                ALU.mult).then_inc(sum_ready[j], 1)
                        pool.wait_ge(sum_ready[j], eval_count(p, s, e))
                        nc.gpsimd.tensor_tensor(v["sum_mean"], v["resid_sum"], moments[:, j, :, 1],
                                                ALU.mult).then_inc(sum_mean_ready[j], 1)
                        pool.wait_ge(sum_mean_ready[j], eval_count(p, s, e))
                        nc.gpsimd.tensor_tensor(v["sq_sum"], v["sum_mean"], moments[:, j, :, 2],
                                                ALU.add).then_inc(sq_ready[j], 1)
                    if stage != "newton":
                        return
                    pool.wait_ge(root_ready[j], eval_count(p, s, e))
                    pool.wait_ge(inv_ready[j], eval_count(p, s, e))
                    nc.gpsimd.tensor_tensor(v["gap"], v["sq_root"], v["sq_sum"], ALU.subtract).then_inc(pool_step[j], 1)
                    pool.wait_ge(pool_step[j], pool_count(p, s, e, 1))
                    nc.gpsimd.tensor_tensor(v["delta"], v["gap"], v["inv_sum"], ALU.mult).then_inc(pool_step[j], 1)
                    pool.wait_ge(pool_step[j], pool_count(p, s, e, 2))
                    if e == 0:
                        nc.gpsimd.tensor_tensor(v["first_delta"], v["delta"], first_scale[:, tag_no, :],
                                                ALU.mult).then_inc(pool_step[j], 1)
                        pool.wait_ge(pool_step[j], pool_count(p, s, e, 3))
                        nc.gpsimd.tensor_tensor(v["neg_u_raw"], neg_u_start[:, tag_no, :], v["first_delta"],
                                                ALU.add).then_inc(pool_step[j], 1)
                    else:
                        nc.gpsimd.tensor_tensor(v["neg_u_raw"], v["neg_u"], v["delta"], ALU.add).then_inc(pool_step[j], 1)
                    if e == evals - 1 and always:
                        pool.wait_ge(pool_step[j], pool_count(p, s, e, 3))
                        nc.gpsimd.tensor_tensor(step2[:, j, :], v["delta"], v["delta"], ALU.mult).then_inc(settle_step[j], 1)
                        pool.wait_ge(settle_step[j], p * (3 * STEPS) + (3 * s + 1))
                        nc.gpsimd.tensor_tensor(step4[:, j, :], step2[:, j, :], step2[:, j, :], ALU.mult).then_inc(settle_step[j], 1)
                        pool.wait_ge(settle_step[j], p * (3 * STEPS) + (3 * s + 2))
                        nc.gpsimd.tensor_tensor(unsettled[:, j, :], unsettled[:, j, :], step4[:, j, :],
                                                ALU.add).then_inc(settle_step[j], 1)
                        pool.wait_ge(settle_step[j], p * (3 * STEPS) + (3 * s + 3))

                pipe.play(pool, run)

            @part(block.tensor)
            def _(pe):
                def run(p, before, j, what):
                    stage, s, e = what
                    if stage == "turn_in":
                        pe.wait_ge(hat_ready[j], p + 1)
                        turn_free(pe, before, 3)
                        for t in range(CT):
                            ins = nc.tensor.transpose(ps_turn_flat[:, P * t:P * (t + 1)], x_hat[:, j, P * t:P * (t + 1)],
                                                      ident[:, :])
                        ins.then_inc(turned_in[j], 1)
                    elif stage == "scores":
                        for q in range(4):
                            if s:
                                pe.wait_ge(turn_emptied[j], turn_count(p, "turn_weights", s - 1, q + 1))
                            elif q == 0:
                                pe.wait_ge(in_emptied[j], p * CT + CT)
                            use = before("scores")
                            if use:
                                pe.wait_ge(scores_used[use[1]], scores_count(use[0], use[2][1], 2 * (q + 1)))
                            for h in (2 * q, 2 * q + 1):
                                for t in range(CT):
                                    lhsT = x_hat_t[:, j, t, :] if s == 0 else weights_t[:, j, h, P * t:P * (t + 1)]
                                    w = score_in_w if s == 0 else score_step_w
                                    ins = nc.tensor.matmul(ps_scores[:, h, :], lhsT, w[:, h, t, :],
                                                           start=(t == 0), stop=(t == CT - 1))
                            ins.then_inc(scores_ready[j], 1)
                    elif stage == "turn_weights":
                        for q in range(4):
                            pe.wait_ge(weights_ready[j], p * (STEPS * 4) + (s * 4 + q + 1))
                            turn_free(pe, before, q)
                            for h in (2 * q, 2 * q + 1):
                                for t in range(NT):
                                    ins = nc.tensor.transpose(ps_turn[:, h, t, :], resid[:, j, h, P * t:P * (t + 1)],
                                                              ident[:, :])
                            ins.then_inc(weights_turned[j], 1)
                    elif stage == "project":
                        turn_free(pe, before, 3)
                        pe.wait_ge(turn_emptied[j], turn_count(p, "turn_weights", STEPS - 1, QUARTERS))
                        for h in range(HEADS):
                            for t in range(NT):
                                ins = nc.tensor.matmul(ps_turn_flat[:, 0:HID], weights_t[:, j, h, P * t:P * (t + 1)],
                                                       value_out_w[:, h, t, :], start=(h == 0 and t == 0),
                                                       stop=(h == HEADS - 1 and t == NT - 1))
                        ins.then_inc(proj_ready[j], 1)
                pipe.play(pe, run)

        with nc.Block() as block:
            memory_attention(block, "quick", **QUICK, always=True)

        with nc.Block() as block:
            @block.vector
            def _(dve):
                nc.vector.tensor_reduce(worst[:, :], unsettled[:, :, :].rearrange("p j h -> p (j h)"), AX_X,
                                        ALU.max).then_inc(flag_step, 1)
                dve.wait_ge(flag_step, 2)
                nc.vector.tensor_scalar(too_far[:, :], worst_all[:, :], LAST_STEP ** 4, None, ALU.is_gt).then_inc(flag_step, 1)
                dve.wait_ge(flag_step, 3)
                nc.vector.tensor_copy(flag[:, :], too_far[:, :]).then_inc(flag_step, 1)

            @block.gpsimd
            def _(pool):
                pool.wait_ge(flag_step, 1)
                nc.gpsimd.partition_all_reduce(worst_all[:, :], worst[:, :], P, RED_MAX).then_inc(flag_step, 1)

        with nc.Block() as block:
            memory_attention(block, "general", **GENERAL, always=False)
        nc.clear_and_free_semaphores(layer_1_sems)
        nc.all_engine_barrier()

        pipe2 = latent_pipeline()
        with ExitStack() as scope, nc.Block() as block:
            (kv_loaded, diag_ready, lat_x_ready, l2_turned, queries_ready, l2_scores_ready, nmax_ready,
             exp_ready, sum_ready, inv_row_ready, probs_ready, probs_turned, contexts_ready, l2_proj_ready,
             q_emptied, s_emptied, p_emptied, c_emptied) = (slot_sems(scope, n) for n in (
                "kv_loaded", "diag_ready", "lat_x_ready", "l2_turned", "queries_ready", "l2_scores_ready", "nmax_ready",
                "exp_ready", "sum_ready", "inv_row_ready", "probs_ready", "probs_turned", "contexts_ready",
                "l2_proj_ready", "q_emptied", "s_emptied", "p_emptied", "c_emptied"))
            diag_zero = sem("diag_zero")

            @block.sync
            def _(sp):
                with sp.Fori(0, PASSES) as p:
                    for j in range(SLOTS):
                        sp.wait_ge(kv_read[j], p + 1)
                        src = ctx_kv.rearrange("b l d -> l b d")[:, bass.ds((p * SLOTS + j) * 2, 2), :]
                        for half in range(2):
                            sp.dma_start(kv_in[64 * half:64 * (half + 1), j, :, :], src).then_inc(kv_loaded[j], 16)

            @block.gpsimd
            def _(pool):
                nc.gpsimd.memset(kv_diag, 0.0).then_inc(diag_zero, 1)
                pool.wait_ge(diag_zero, 1)
                H = XD // 2

                def run(p, before, j, what):
                    stage = what[0]
                    if stage == "fetch":
                        pool.wait_ge(kv_loaded[j], p * 32 + 32)
                        nc.gpsimd.tensor_tensor(kv_cos[:, j, :, :], kv_in[:, j, :, :], cos_sb[:, :, :], ALU.mult)
                        nc.gpsimd.tensor_tensor(kv_rot[:, j, :, 0:H], kv_in[:, j, :, H:XD], sin_sb[:, :, 0:H], ALU.mult)
                        nc.gpsimd.tensor_tensor(kv_rot[:, j, :, H:XD], kv_in[:, j, :, 0:H], sin_sb[:, :, H:XD],
                                                ALU.mult).then_inc(kv_read[j], 1)
                        pool.wait_ge(kv_read[j], p + 2)
                        for half in range(2):
                            at = slice(64 * half, 64 * (half + 1))
                            nc.gpsimd.tensor_tensor(kv_diag[at, j, :, XD * half:XD * (half + 1)], kv_cos[at, j, :, :],
                                                    kv_rot[at, j, :, :], ALU.add).then_inc(diag_ready[j], 1)
                            pool.wait_ge(diag_ready[j], p * 2 + (half + 1))
                    elif stage == "normalise":
                        pool.wait_ge(inv_row_ready[j], p + 1)
                        nc.gpsimd.tensor_tensor(probs[:, j, :, :], probs[:, j, :, :],
                                                row_inv[:, j, :].unsqueeze(2).to_broadcast([P, XH, XD]),
                                                ALU.mult).then_inc(probs_ready[j], 1)
                    elif stage == "residual":
                        store_row(pool, row_summed, row_stored, p * SLOTS + j, p + PASSES, j)
                pipe2.play(pool, run)

            @block.scalar
            def _(act):
                row_roots(act, 1, tile_var_ready, tile_std_ready)

                def run(p, before, j, what):
                    stage = what[0]
                    if stage == "turn_x":
                        act.wait_ge(l2_turned[j], p + 1)
                        nc.scalar.activation(lat_x_t[:, j, :, :], pl_q[:, 0:2, :], ACT.Copy).then_inc(q_emptied[j], 1)
                        nc.scalar.activation(kv_diag_t[:, j, :, :], pl_q[:, 2:4, :], ACT.Copy).then_inc(q_emptied[j], 1)
                    elif stage == "queries":
                        for q in range(2):
                            act.wait_ge(queries_ready[j], p * 2 + (q + 1))
                            nc.scalar.activation(lat_q_t[:, j, 4 * q:4 * q + 4, :], pl_q[:, 4 * q:4 * q + 4, :],
                                                 ACT.Copy).then_inc(q_emptied[j], 1)
                    elif stage == "exp":
                        act.wait_ge(s_emptied[j], p + 1)
                        nc.scalar.activation(probs[:, j, :, :], probs[:, j, :, :], ACT.Exp).then_inc(exp_ready[j], 1)
                    elif stage == "turn_probs":
                        for q in range(2):
                            act.wait_ge(probs_turned[j], p * 2 + (q + 1))
                            nc.scalar.activation(probs_t[:, j, 4 * q:4 * q + 4, :], pl_p[:, 4 * q:4 * q + 4, :],
                                                 ACT.Copy).then_inc(p_emptied[j], 1)
                pipe2.play(act, run)

            @block.vector
            def _(dve):
                row_norms(dve, 1, norm_step, tile_var_ready, tile_std_ready)

                def run(p, before, j, what):
                    stage = what[0]
                    if stage == "fetch":
                        src, mean, rstd = at_tile(p * SLOTS + j)
                        nc.vector.tensor_scalar(lat_x[:, j, :], src, mean, rstd, ALU.subtract, ALU.mult).then_inc(lat_x_ready[j], 1)
                    elif stage == "shift":
                        dve.wait_ge(l2_scores_ready[j], p + 1)
                        nc.vector.tensor_reduce(row_nmax[:, j, :], pl_s, AX_X, ALU.max, negate=True).then_inc(nmax_ready[j], 1)
                        dve.wait_ge(nmax_ready[j], p + 1)
                        nc.vector.tensor_tensor(probs[:, j, :, :], pl_s,
                                                row_nmax[:, j, :].unsqueeze(2).to_broadcast([P, XH, XD]),
                                                ALU.add).then_inc(s_emptied[j], 1)
                    elif stage == "sum":
                        dve.wait_ge(exp_ready[j], p + 1)
                        nc.vector.tensor_reduce(row_sum[:, j, :], probs[:, j, :, :], AX_X, ALU.add).then_inc(sum_ready[j], 1)
                        dve.wait_ge(sum_ready[j], p + 1)
                        nc.vector.reciprocal(row_inv[:, j, :], row_sum[:, j, :]).then_inc(inv_row_ready[j], 1)
                    elif stage == "contexts":
                        dve.wait_ge(contexts_ready[j], p + 1)
                        nc.vector.tensor_copy(lat_c_t[:, j, :, :], pl_c).then_inc(c_emptied[j], 1)
                    elif stage == "residual":
                        dve.wait_ge(l2_proj_ready[j], p + 1)
                        dve.wait_ge(row_stored[j], p * 2 + (2 * PASSES + 2))
                        nc.vector.tensor_tensor(y_row[:, j, :], pl_c[:, 0:2, :].rearrange("p a b -> p (a b)"),
                                                lat_x[:, j, :], ALU.add).then_inc(c_emptied[j], 1)
                        dve.wait_ge(c_emptied[j], p * 2 + 2)
                        nc.vector.bn_stats(stats[:, j, :], y_row[:, j, :]).then_inc(row_summed[j], 1)
                pipe2.play(dve, run)

            @block.tensor
            def _(pe):
                def free(before, sems, counts):
                    use = before(*counts)
                    if use:
                        p, j, what = use
                        pe.wait_ge(sems[j], p * max(counts.values()) + counts[what[0]])

                def run(p, before, j, what):
                    stage = what[0]
                    if stage == "turn_x":
                        pe.wait_ge(lat_x_ready[j], p + 1)
                        pe.wait_ge(diag_ready[j], p * 2 + 2)
                        free(before, q_emptied, {"turn_x": 2, "queries": 4})
                        for t in range(CT):
                            nc.tensor.transpose(pl_q[:, t, :], lat_x[:, j, P * t:P * (t + 1)], ident[:, :])
                        for b in range(2):
                            ins = nc.tensor.transpose(pl_q[:, 2 + b, :], kv_diag[:, j, b, :], ident[:, :])
                        ins.then_inc(l2_turned[j], 1)
                    elif stage == "queries":
                        free(before, q_emptied, {"turn_x": 2, "queries": 4})
                        pe.wait_ge(q_emptied[j], p * 4 + 2)
                        for g in range(PAIRS):
                            for t in range(CT):
                                ins = nc.tensor.matmul(pl_q[:, g, :], latent_q_w[:, t, P * g:P * (g + 1)],
                                                       lat_x_t[:, j, t, :], start=(t == 0), stop=(t == CT - 1))
                            if g % 4 == 3:
                                ins.then_inc(queries_ready[j], 1)
                    elif stage == "scores":
                        pe.wait_ge(q_emptied[j], p * 4 + 4)
                        free(before, s_emptied, {"scores": 1})
                        for g in range(PAIRS):
                            for b in range(2):
                                at = slice(64 * b, 64 * (b + 1))
                                ins = nc.tensor.matmul(pl_s[at, 2 * g:2 * g + 2, :], lat_q_t[:, j, g, at],
                                                       kv_diag_t[:, j, b, :], start=True, stop=True)
                        ins.then_inc(l2_scores_ready[j], 1)
                    elif stage == "turn_probs":
                        pe.wait_ge(probs_ready[j], p + 1)
                        free(before, p_emptied, {"turn_probs": 2})
                        for g in range(PAIRS):
                            ins = nc.tensor.transpose(pl_p[:, g, :], probs[:, j, 2 * g:2 * g + 2, :]
                                                      .rearrange("p h l -> p (h l)"), ident[:, :])
                            if g % 4 == 3:
                                ins.then_inc(probs_turned[j], 1)
                    elif stage == "contexts":
                        pe.wait_ge(p_emptied[j], p * 2 + 2)
                        free(before, c_emptied, {"contexts": 1, "project": 2})
                        for g in range(PAIRS):
                            for b in range(2):
                                at = slice(64 * b, 64 * (b + 1))
                                ins = nc.tensor.matmul(pl_c[:, g, at], kv_diag[:, j, b, :], probs_t[:, j, g, at],
                                                       start=True, stop=True)
                        ins.then_inc(contexts_ready[j], 1)
                    elif stage == "project":
                        pe.wait_ge(c_emptied[j], p * 2 + 1)
                        free(before, c_emptied, {"contexts": 1, "project": 2})
                        for g in range(PAIRS):
                            ins = nc.tensor.matmul(pl_c[:, 0:2, :], lat_c_t[:, j, g, :], latent_o_w[:, g, :],
                                                   start=(g == 0), stop=(g == PAIRS - 1))
                        ins.then_inc(l2_proj_ready[j], 1)
                pipe2.play(pe, run)

        pipe3 = dense_pipeline()
        with ExitStack() as scope, nc.Block() as block:
            x2_ready, biased, l3_turned, x2_t_ready, dense_ready, dense_read, out_ready, stored = (slot_sems(scope, n) for n in
                ("x2_ready", "biased", "l3_turned", "x2_t_ready", "dense_ready", "dense_read", "out_ready", "stored"))

            @block.scalar
            def _(act):
                row_roots(act, 2, tile_var_ready, tile_std_ready)

                def run(p, before, j, what):
                    if what[0] == "turn":
                        act.wait_ge(l3_turned[j], p + 1)
                        nc.scalar.activation(x2_t[:, j, :, :], pd_turn[j], ACT.Copy).then_inc(x2_t_ready[j], 1)
                pipe3.play(act, run)
                row_roots(act, 3, tile_var_ready, tile_std_ready)

            @block.vector
            def _(dve):
                row_norms(dve, 2, norm_step, tile_var_ready, tile_std_ready)

                def run(p, before, j, what):
                    if what[0] == "norm_in":
                        src, mean, rstd = at_tile(p * SLOTS + j)
                        nc.vector.tensor_scalar(x2[:, j, :], src, mean, rstd, ALU.subtract, ALU.mult).then_inc(x2_ready[j], 1)
                    elif what[0] == "residual":
                        dve.wait_ge(dense_ready[j], p + 1)
                        dve.wait_ge(row_stored[j], p * 2 + (4 * PASSES + 2))
                        dve.wait_ge(biased[j], p + 1)
                        nc.vector.tensor_tensor(y_row[:, j, :], pd_dense[j], x2_bias[:, j, :], ALU.add).then_inc(dense_read[j], 1)
                        nc.vector.tensor_tensor(at_tile(p * SLOTS + j)[0], pd_dense[j], x2_bias[:, j, :],
                                                ALU.add).then_inc(row_stored[j], 1)
                        dve.wait_ge(dense_read[j], p + 1)
                        nc.vector.bn_stats(stats[:, j, :], y_row[:, j, :]).then_inc(row_summed[j], 1)
                pipe3.play(dve, run)
                for j in range(SLOTS):
                    dve.wait_ge(row_stored[j], 6 * PASSES + 2)
                row_norms(dve, 3, norm_step, tile_var_ready, tile_std_ready)
                with dve.Fori(0, PASSES) as p:
                    for j in range(SLOTS):
                        src, mean, rstd = at_tile(p * SLOTS + j)
                        dve.wait_ge(stored[j], p * 16 + 16)
                        nc.vector.tensor_scalar(out_row[:, j, :], src, mean, rstd, ALU.subtract, ALU.mult).then_inc(out_ready[j], 1)

            @block.gpsimd
            def _(pool):
                def run(p, before, j, what):
                    if what[0] == "turn":
                        pool.wait_ge(x2_ready[j], p + 1)
                        nc.gpsimd.tensor_tensor(x2_bias[:, j, :], x2[:, j, :], bias_rows[:, :], ALU.add).then_inc(biased[j], 1)
                    elif what[0] == "residual":
                        store_stats(pool, row_summed, row_stored, p * SLOTS + j, p + 2 * PASSES, j)
                pipe3.play(pool, run)

            @block.tensor
            def _(pe):
                def run(p, before, j, what):
                    if what[0] == "turn":
                        pe.wait_ge(x2_ready[j], p + 1)
                        for t in range(CT):
                            ins = nc.tensor.transpose(pd_turn[j][:, t, :], x2[:, j, P * t:P * (t + 1)], ident[:, :])
                        ins.then_inc(l3_turned[j], 1)
                    elif what[0] == "dense":
                        pe.wait_ge(x2_t_ready[j], p + 1)
                        for t in range(CT):
                            ins = nc.tensor.matmul(pd_dense[j], x2_t[:, j, t, :], ffn_wt[:, t, :], start=(t == 0),
                                                   stop=(t == CT - 1))
                        ins.then_inc(dense_ready[j], 1)
                pipe3.play(pe, run)

            @block.sync
            def _(sp):
                for j in range(SLOTS):
                    sp.sem_inc(stored[j], 16)
                with sp.Fori(0, PASSES) as p:
                    for j in range(SLOTS):
                        sp.wait_ge(out_ready[j], p + 1)
                        sp.dma_start(out[bass.ds((p * SLOTS + j) * P, P), :], out_row[:, j, :]).then_inc(stored[j], 16)
                for j in range(SLOTS):
                    sp.wait_ge(stored[j], 16 * (PASSES + 1))


_INS = ["x", "ctx_512", "L0_attn_memory", "L0_attn_Wq", "L0_attn_Wk", "L0_attn_Wv", "L0_attn_Wo", "L0_attn_log_beta",
        "L0_attn_g_state", "L0_attn_b_state", "L0_attn_g_mem", "L0_attn_b_mem", "L0_xattn_Wq", "L0_xattn_w_kc_q",
        "L0_xattn_w_kc_kv", "L0_xattn_W_qr", "L0_xattn_W_kr", "L0_xattn_Wo", "L0_ffn_weight", "L0_ffn_scale_weight",
        "L0_ffn_bias"]


def rope_tables():
    import numpy as np
    inv_freq = (1.0 / np.float32(10000.0) ** (np.arange(0, XD, 2, dtype=np.float32) / np.float32(XD))).astype(np.float32)
    freqs = np.arange(SEQ, dtype=np.float32)[:, None] * inv_freq[None, :]
    cos = np.repeat(np.cos(freqs), 2, axis=-1)
    sin = np.repeat(np.sin(freqs), 2, axis=-1)
    sin[:, :XD // 2] *= -1.0
    return [np.ascontiguousarray(np.tile(t.astype(np.float32), (2, 2))) for t in (cos, sin)]


def kernel(**inputs):
    import numpy as np
    import concourse.bacc as bacc
    from concourse.bass_utils import run_bass_kernel_spmd

    nc = bacc.Bacc("TRN2", target_bir_lowering=False, num_devices=1)
    nc.disable_value_cache = True
    arrays, args = {}, []

    def add(name, a):
        arrays[f"in_{name}_dram"] = a
        args.append(nc.dram_tensor(f"in_{name}_dram", a.shape, mybir.dt.from_np(a.dtype), kind="ExternalInput").ap())

    for name in _INS:
        a = np.ascontiguousarray(inputs[name])
        add(name, a.reshape(ROWS, HID) if name == "x" else a)
    cos, sin = rope_tables()
    add("rope_cos", cos)
    add("rope_sin", sin)
    out = nc.dram_tensor("out_0_dram", (ROWS, HID), F32, kind="ExternalOutput").ap()
    decoder_kernel(nc, *args, out)
    r = run_bass_kernel_spmd(nc, [arrays], core_ids=[0])
    return r.results[0]["out_0_dram"].reshape(BATCH, SEQ, HID)
```
